# Optimizing a Trainium2 kernel written in Bass

```python
import numpy as np
import jax
import jax.numpy as jnp

def _softmax(x, axis=-1):
    return jax.nn.softmax(x, axis=axis)

def _gelu(x):
    return jax.nn.gelu(x, approximate=True)

def _silu(x):
    return jax.nn.silu(x)

def _sigmoid(x):
    return jax.nn.sigmoid(x)

def _layernorm(x, axis=-1, eps=1e-05):
    m = jnp.mean(x, axis=axis, keepdims=True)
    v = jnp.var(x, axis=axis, keepdims=True)
    return (x - m) / jnp.sqrt(v + eps)

def _scatter_add(tgt, idx, src, axis=0):
    return tgt.at[idx].add(src)

def _segment_sum(src, seg, n):
    return jax.ops.segment_sum(src, seg, n)
kernel_name = 'mk_xattn_seq_d2_seqx_r8_763145'

def setup_inputs(seed: int=0):
    np.random.seed(seed)
    _w = jnp.asarray

    def _rec_inputs():
        import jax
        import jax.numpy as jnp
        _rk = jax.random.key(seed)
        x = -0.000296 + 1 * jax.random.normal(jax.random.fold_in(_rk, 1), (8, 256, 160), jnp.float32)
        _lenS = 256 - jax.random.randint(jax.random.fold_in(_rk, 7), (8,), 0, max(1, 256 // 4) + 1, jnp.int32)
        _lenS2 = 512 - jax.random.randint(jax.random.fold_in(_rk, 8), (8,), 0, max(1, 512 // 4) + 1, jnp.int32)
        _ctx_2048P = jax.random.normal(jax.random.fold_in(_rk, 11), (8, 16, 256), jnp.float32)
        _ctx_2048c = jax.random.dirichlet(jax.random.fold_in(_rk, 511), 0.3 * jnp.ones((16,), jnp.float32), (8, 512))
        _ctx_2048t = jnp.einsum('bsk,bkd->bsd', _ctx_2048c, _ctx_2048P)
        _ctx_2048t = _ctx_2048t * jax.lax.rsqrt(jnp.mean(jnp.square(_ctx_2048t)) + 1e-12) * 0.953939
        ctx_2048 = 0.00100794 + 0.99956 * (_ctx_2048t + 0.3 * jax.random.normal(jax.random.fold_in(_rk, 611), (8, 512, 256), jnp.float32))
        fside_S_0 = jax.random.uniform(jax.random.fold_in(_rk, 12), (256,), jnp.float32, 0.0, 0.999707)
        return (x, ctx_2048, fside_S_0)
    x, ctx_2048, fside_S_0 = _rec_inputs()

    def _L0_xattn_setup():
        import jax, jax.numpy as jnp
        import numpy as np
        import math
        HEADS = 20
        NUM_TOKENS = 4
        SEM_SCALE = 0.5
        IP_SCALE = 1.0
        TEXT_LEN = 77

        def _split_heads(x, B, H, D):
            return x.reshape(B, -1, H, D).transpose(0, 2, 1, 3)
        key = jax.random.key(seed)
        ks = jax.random.split(key, 10)
        B, S, C, CD = (4, 512, 160, 256)

        def g(k, shape, std=1.0):
            return jax.random.normal(k, shape, dtype=jnp.float32) * std
        return {'hidden_states': g(ks[0], (B, S, C)), 'encoder_hidden_states': g(ks[1], (B, TEXT_LEN + NUM_TOKENS, CD)), 'spatial_mask': jax.random.uniform(ks[2], (S,), dtype=jnp.float32), 'Wq': g(ks[3], (C, C), 1.0 / math.sqrt(C)), 'Wk': g(ks[4], (CD, C), 1.0 / math.sqrt(CD)), 'Wv': g(ks[5], (CD, C), 1.0 / math.sqrt(CD)), 'Wk_ip': g(ks[6], (CD, C), 1.0 / math.sqrt(CD)), 'Wv_ip': g(ks[7], (CD, C), 1.0 / math.sqrt(CD)), 'Wout': g(ks[8], (C, C), 1.0 / math.sqrt(C)), 'bout': jnp.zeros((C,), dtype=jnp.float32)}
    _L0_xattn_all = _L0_xattn_setup()
    _L0_xattn_in = {k: v for k, v in _L0_xattn_all.items() if k in ('Wq', 'Wk', 'Wv', 'Wk_ip', 'Wv_ip', 'Wout', 'bout')}
    del _L0_xattn_all

    def _L1_xattn_setup():
        import jax, jax.numpy as jnp
        import numpy as np
        NUM_HEADS = 20
        TEXT_LEN = 77
        IP_SCALE = 1.0

        def _attend(q, k, v, sm_scale):
            scores = jnp.einsum('bhsd,bhld->bhsl', q, k) * sm_scale
            probs = jax.nn.softmax(scores, axis=-1)
            return jnp.einsum('bhsl,bhld->bhsd', probs, v)

        def _split_heads(x, h):
            b, s, c = x.shape
            return x.reshape(b, s, h, c // h).transpose(0, 2, 1, 3)

        def _merge_heads(x):
            b, h, s, d = x.shape
            return x.transpose(0, 2, 1, 3).reshape(b, s, h * d)
        key = jax.random.key(seed)
        ks = jax.random.split(key, 8)
        B, S, C, CC, L = (8, 512, 160, 256, TEXT_LEN + 4)
        sd_q = 1.0 / np.sqrt(C)
        sd_kv = 1.0 / np.sqrt(CC)
        return {'hidden_states': jax.random.normal(ks[0], (B, S, C), jnp.float32), 'encoder_hidden_states': jax.random.normal(ks[1], (B, L, CC), jnp.float32), 'Wq': jax.random.normal(ks[2], (C, C), jnp.float32) * sd_q, 'Wk': jax.random.normal(ks[3], (C, CC), jnp.float32) * sd_kv, 'Wv': jax.random.normal(ks[4], (C, CC), jnp.float32) * sd_kv, 'Wk_ip': jax.random.normal(ks[5], (C, CC), jnp.float32) * sd_kv, 'Wv_ip': jax.random.normal(ks[6], (C, CC), jnp.float32) * sd_kv, 'Wo': jax.random.normal(ks[7], (C, C), jnp.float32) * sd_q, 'bo': jnp.zeros((C,), jnp.float32)}
    _L1_xattn_all = _L1_xattn_setup()
    _L1_xattn_in = {k: v for k, v in _L1_xattn_all.items() if k in ('Wq', 'Wk', 'Wv', 'Wk_ip', 'Wv_ip', 'Wo', 'bo')}
    del _L1_xattn_all
    return {'x': x, 'ctx_2048': ctx_2048, 'fside_S_0': fside_S_0, 'L0_xattn_Wq': _L0_xattn_in['Wq'], 'L0_xattn_Wk': _L0_xattn_in['Wk'], 'L0_xattn_Wv': _L0_xattn_in['Wv'], 'L0_xattn_Wk_ip': _L0_xattn_in['Wk_ip'], 'L0_xattn_Wv_ip': _L0_xattn_in['Wv_ip'], 'L0_xattn_Wout': _L0_xattn_in['Wout'], 'L0_xattn_bout': _L0_xattn_in['bout'], 'L1_xattn_Wq': _L1_xattn_in['Wq'], 'L1_xattn_Wk': _L1_xattn_in['Wk'], 'L1_xattn_Wv': _L1_xattn_in['Wv'], 'L1_xattn_Wk_ip': _L1_xattn_in['Wk_ip'], 'L1_xattn_Wv_ip': _L1_xattn_in['Wv_ip'], 'L1_xattn_Wo': _L1_xattn_in['Wo'], 'L1_xattn_bo': _L1_xattn_in['bo']}

def reference(x, ctx_2048, fside_S_0, L0_xattn_Wq, L0_xattn_Wk, L0_xattn_Wv, L0_xattn_Wk_ip, L0_xattn_Wv_ip, L0_xattn_Wout, L0_xattn_bout, L1_xattn_Wq, L1_xattn_Wk, L1_xattn_Wv, L1_xattn_Wk_ip, L1_xattn_Wv_ip, L1_xattn_Wo, L1_xattn_bo):
    import jax
    import jax.numpy as jnp

    def _L0_xattn_ref(hidden_states, encoder_hidden_states, spatial_mask, Wq, Wk, Wv, Wk_ip, Wv_ip, Wout, bout):
        import jax, jax.numpy as jnp
        import numpy as np
        import math
        HEADS = 20
        NUM_TOKENS = 4
        SEM_SCALE = 0.5
        IP_SCALE = 1.0
        TEXT_LEN = 77

        def _split_heads(x, B, H, D):
            return x.reshape(B, -1, H, D).transpose(0, 2, 1, 3)
        B, S, C = hidden_states.shape
        D = C // HEADS
        scale = 1.0 / math.sqrt(D)
        residual = hidden_states
        text = encoder_hidden_states[:, :TEXT_LEN]
        ip = encoder_hidden_states[:, TEXT_LEN:]
        q = hidden_states @ Wq
        k_text = text @ Wk
        v_text = text @ Wv
        q_h = _split_heads(q, B, HEADS, D)
        k_h = _split_heads(k_text, B, HEADS, D)
        v_h = _split_heads(v_text, B, HEADS, D)
        logits = jnp.einsum('bhqd,bhkd->bhqk', q_h, k_h) * scale
        probs = jax.nn.softmax(logits, axis=-1)
        text_out = jnp.einsum('bhqk,bhkd->bhqd', probs, v_h)
        text_out = text_out.transpose(0, 2, 1, 3).reshape(B, S, C)
        ip_k = ip @ Wk_ip
        ip_v = ip @ Wv_ip
        ip_k_h = _split_heads(ip_k, B, HEADS, D)
        ip_v_h = _split_heads(ip_v, B, HEADS, D)
        scores = jnp.einsum('bhqd,bhkd->bhqk', q_h, ip_k_h) * scale
        text_probs = jax.nn.softmax(jnp.einsum('bqc,bkc->bqk', q, k_text) * scale, axis=-1)
        q_sem = jnp.einsum('bqk,bkc->bqc', text_probs, text)
        sem = jnp.einsum('bqc,bnc->bqn', q_sem, ip) * scale
        sem = jax.lax.stop_gradient(sem)
        fused = scores + SEM_SCALE * sem[:, None, :, :]
        ip_probs = jax.nn.softmax(fused, axis=-1)
        ip_probs = ip_probs * spatial_mask[None, None, :, None]
        ip_out = jnp.einsum('bhqk,bhkd->bhqd', ip_probs, ip_v_h)
        ip_out = ip_out.transpose(0, 2, 1, 3).reshape(B, S, C)
        hs = text_out + IP_SCALE * ip_out
        out = hs @ Wout + bout
        out = out + residual
        return out

    def _L1_xattn_ref(hidden_states, encoder_hidden_states, Wq, Wk, Wv, Wk_ip, Wv_ip, Wo, bo):
        import jax, jax.numpy as jnp
        import numpy as np
        NUM_HEADS = 20
        TEXT_LEN = 77
        IP_SCALE = 1.0

        def _attend(q, k, v, sm_scale):
            scores = jnp.einsum('bhsd,bhld->bhsl', q, k) * sm_scale
            probs = jax.nn.softmax(scores, axis=-1)
            return jnp.einsum('bhsl,bhld->bhsd', probs, v)

        def _split_heads(x, h):
            b, s, c = x.shape
            return x.reshape(b, s, h, c // h).transpose(0, 2, 1, 3)

        def _merge_heads(x):
            b, h, s, d = x.shape
            return x.transpose(0, 2, 1, 3).reshape(b, s, h * d)
        residual = hidden_states
        B, S, C = hidden_states.shape
        H = NUM_HEADS
        D = C // H
        sm_scale = 1.0 / jnp.sqrt(jnp.asarray(D, hidden_states.dtype))
        text = encoder_hidden_states[:, :TEXT_LEN, :]
        ip = encoder_hidden_states[:, TEXT_LEN:, :]
        q = _split_heads(hidden_states @ Wq.T, H)
        k = _split_heads(text @ Wk.T, H)
        v = _split_heads(text @ Wv.T, H)
        out_text = _merge_heads(_attend(q, k, v, sm_scale))
        k_ip = _split_heads(ip @ Wk_ip.T, H)
        v_ip = _split_heads(ip @ Wv_ip.T, H)
        out_ip = _merge_heads(_attend(q, k_ip, v_ip, sm_scale))
        out = out_text + IP_SCALE * out_ip
        out = out @ Wo.T + bo
        return out + residual
    x = _L0_xattn_ref(x, ctx_2048, fside_S_0, L0_xattn_Wq, L0_xattn_Wk, L0_xattn_Wv, L0_xattn_Wk_ip, L0_xattn_Wv_ip, L0_xattn_Wout, L0_xattn_bout)
    x = _L1_xattn_ref(x, ctx_2048, L1_xattn_Wq, L1_xattn_Wk, L1_xattn_Wv, L1_xattn_Wk_ip, L1_xattn_Wv_ip, L1_xattn_Wo, L1_xattn_bo)
    return x

_drawn_inputs = setup_inputs


def setup_inputs(seed=0):
    import zlib

    import numpy as np

    out = dict(_drawn_inputs(seed))
    spreads = {'L0_xattn_bout': (0.0, 0.1), 'L1_xattn_bo': (0.0, 0.1)}
    factors = {}
    for name, (base, spread) in spreads.items():
        noise = np.random.default_rng([zlib.crc32(name.encode()), seed]).standard_normal(out[name].shape)
        drawn = base * np.exp(spread * noise) if base else spread * noise
        out[name] = jnp.asarray(drawn.astype(out[name].dtype))
    for name, factor in factors.items():
        out[name] = (out[name] * factor).astype(out[name].dtype)
    return out
```

```python
from contextlib import ExitStack

import concourse.bass as bass
from concourse import mybir

F32 = mybir.dt.float32
BF16 = mybir.dt.bfloat16
ACT = mybir.ActivationFunctionType
ALU = mybir.AluOpType
AX = mybir.AxisListType.X

B, S, C, CD, L, T = 8, 256, 160, 256, 512, 77
H = 20
D = C // H
SCALE = float(D) ** -0.5
SEM_SCALE = 0.5
P = 128
LAYERS = 2
ITEMS = LAYERS * B
HG = 4
NG = H // HG
QT = S // P
KC = L // P
PARTS = 3
STACK = PARTS * PARTS * D
MROW = 96
MR = 2 * PARTS
KROWS = MROW + MR
RING = 10
FUSED = 4
VW = 32
IPC = 9


class Signal:

    def __init__(self, sem, per, unit=1):
        self.sem, self.per, self.unit = sem, per, unit

    def start(self, eng):
        eng.sem_inc(self.sem, self.per * self.unit)

    def at(self, turn, count):
        return turn * (self.per * self.unit) + (self.per + count) * self.unit


def build(nc, xT, ctxT, mask, wk_text, wk_ip, wv_text, wv_ip, wq, wo, bo,
          ident, key_kind, value_ones, den_of, first_rows, out):
    k_stack = nc.dram_tensor("k_stack", (LAYERS, B, PARTS, PARTS, D * H, L), BF16, kind="Internal").ap()
    q_stack = nc.dram_tensor("q_stack", (LAYERS, B, PARTS, PARTS, D * H, S), BF16, kind="Internal").ap()
    sem_q_dram = nc.dram_tensor("sem_q_dram", (B, P, QT, L - T), F32, kind="Internal").ap()
    sem_k_dram = nc.dram_tensor("sem_k_dram", (B, P, PARTS, KC * S), BF16, kind="Internal").ap()
    x1_dram = nc.dram_tensor("x1_dram", (B, C, S), F32, kind="Internal").ap()
    CT = C - P

    with ExitStack() as ctx:
        def sb(name, shape, dt=F32):
            return ctx.enter_context(nc.sbuf_tensor(name, shape, dt))

        def sem(name):
            return ctx.enter_context(nc.semaphore(name))

        wkt = sb("wkt", [P, 2, 3 * P])
        wki = sb("wki", [P, 2, 3 * P])
        wvt = sb("wvt", [P, 2, LAYERS * C])
        wvi = sb("wvi", [P, 2, LAYERS * C])
        wq_sb = sb("wq_sb", [P, LAYERS, 2, 2 * P])
        wo_sb = sb("wo_sb", [P, LAYERS, NG, C])
        bo_sb = sb("bo_sb", [P, LAYERS, 2])
        id_f = sb("id_f", [P, P])
        id_b = sb("id_b", [P, P], BF16)
        den_sb = sb("den_sb", [P, P])
        rows_sb = sb("rows_sb", [P, 2])
        mask_sb = sb("mask_sb", [P, S])
        ctx_sb = sb("ctx_sb", [P, 2, L])
        x_sb = sb("x_sb", [P, 2, S])
        kt32 = sb("kt32", [P, 2, T])
        qt32 = sb("qt32", [P, 2, S])
        gram = sb("gram", [T, L])
        e_txt = sb("e_txt", [P, QT, T])
        p_txt = sb("p_txt", [P, QT, T])
        pT_txt = sb("pT_txt", [T, S])
        stat = sb("stat", [P, 4, QT])
        ks = sb("ks", [P, NG, HG, L], BF16)
        qs = sb("qs", [P, NG, HG, S], BF16)
        vals = sb("vals", [P, LAYERS, B, KC + 1, C])
        vtile = sb("vtile", [P, NG, KC, HG, VW])
        probs = sb("probs", [P, RING, KC * S])
        sem_q = sb("sem_q", [P, QT, L - T])
        sem_k = sb("sem_k", [P, PARTS, KC * S], BF16)
        fused = sb("fused", [P, FUSED, L - T], BF16)
        mx = sb("mx", [P, NG, QT, 2, HG])
        mres = sb("mres", [P, QT, 2, HG])
        mpart = sb("mpart", [P, QT, 2, PARTS, HG], BF16)
        mrow = sb("mrow", [MR * HG, S], BF16)
        pv_sb = sb("pv_sb", [P, S])
        inv = sb("inv", [P, S])
        hs = sb("hs", [P, NG, S])
        res = sb("res", [P, 2, S])
        y_sb = sb("y_sb", [P, 2, S])
        q_parts = sb("q_parts", [P, PARTS, 2 * S], BF16)
        q_rest = sb("q_rest", [P, 2 * S])

        UNITS = ["k0", "krem", "q", "k1", "s0", "s1"]
        flat = probs[:, :, :].rearrange("p a b -> p (a b)")
        half = PARTS * L // 2
        parts = [flat[:, u * half:(u + 1) * half].bitcast(BF16).rearrange("p (a b) -> p a b", a=PARTS)
                 for u in range(6)]
        rest = [flat[:, 6 * half + u * L:6 * half + (u + 1) * L] for u in range(6)]

        bank = [ctx.enter_context(nc.psum_tensor(f"bank{i}", [P, 512], F32)) for i in range(2)]
        sc = [ctx.enter_context(nc.psum_tensor(f"by_key{i}", [P, 2, 512], F32)) for i in range(2)]
        pv_bank = ctx.enter_context(nc.psum_tensor("pv_bank", [P, 512], F32))
        misc = ctx.enter_context(nc.psum_tensor("misc", [P, 512], F32))
        pbank = [sc[0][:, 0, :], sc[0][:, 1, :], sc[1][:, 0, :], sc[1][:, 1, :],
                 bank[0][:, :], bank[1][:, :], pv_bank[:, :], misc[:, :]]

        consts_in = sem("consts_in")
        init_done = sem("init_done")
        kinds_in = sem("kinds_in")
        id_b_ready = sem("id_b_ready")
        waited_pool = sem("waited_pool")
        waited_dve = sem("waited_dve")
        ctx_in = Signal(sem("ctx_in"), 2, 16)
        x_in = Signal(sem("x_in"), 2, 16)
        products = Signal(sem("products"), 16)
        act_prep = Signal(sem("act_prep"), 18)
        dve_prep = Signal(sem("dve_prep"), 13)
        split_done = Signal(sem("split_done"), 12)
        unit_stored = [Signal(sem(f"stored_{u}"), k, 16) for u, k in zip(UNITS, (3, 6, 6, 3, 1, 1))]
        sem_q_stored = Signal(sem("sem_q_stored"), 1, 16)
        prep_signals = [ctx_in, x_in, products, act_prep, dve_prep, split_done, sem_q_stored, *unit_stored]
        kq_in = [Signal(sem(f"kq_in{g}"), 2, 16) for g in range(NG)]
        a_ready = Signal(sem("a_ready"), 2 * H)
        a_taken = Signal(sem("a_taken"), 2 * H)
        m_split = Signal(sem("m_split"), 4 * NG)
        m_turned = Signal(sem("m_turned"), NG)
        m_row_out = Signal(sem("m_row_out"), NG)
        m_row_in = Signal(sem("m_row_in"), HG * NG, 16)
        s_ready = Signal(sem("s_ready"), H)
        probs_ready = Signal(sem("probs_ready"), H)
        v_placed = Signal(sem("v_placed"), NG)
        pv_ready = Signal(sem("pv_ready"), NG)
        pv_copied = Signal(sem("pv_copied"), NG)
        den_ready = Signal(sem("den_ready"), NG)
        inv_ready = Signal(sem("inv_ready"), NG)
        hs_unmasked = Signal(sem("hs_unmasked"), NG)
        hs_ready = Signal(sem("hs_ready"), NG)
        sem_q_in = Signal(sem("sem_q_in"), 1, 16)
        sem_k_in = Signal(sem("sem_k_in"), 1, 16)
        res_in = Signal(sem("res_in"), 2, 16)
        y_mm = Signal(sem("y_mm"), 1)
        y_ready = Signal(sem("y_ready"), 2)
        y_stored = Signal(sem("y_stored"), 2, 16)
        q1_mm = Signal(sem("q1_mm"), 1)
        q1_hi = Signal(sem("q1_hi"), 1)
        q1_rest = Signal(sem("q1_rest"), 1)
        q1_split = Signal(sem("q1_split"), 2)
        q1_stored = Signal(sem("q1_stored"), 6, 16)
        pe_signals = [a_ready, m_turned, s_ready, pv_ready, den_ready, y_mm, q1_mm, products]
        act_signals = [act_prep, m_row_out, probs_ready, pv_copied, q1_hi]
        dve_signals = [dve_prep, a_taken, inv_ready, y_ready, q1_rest]
        pool_signals = [split_done, m_split, v_placed, hs_unmasked, hs_ready, q1_split]
        dma_signals = [ctx_in, x_in, *unit_stored, sem_q_stored, *kq_in, m_row_in, sem_q_in, sem_k_in,
                       res_in, y_stored, q1_stored]

        N_CONST = 7 + 5 * LAYERS + HG
        pe_job = {n: i + 1 for i, n in enumerate(
            ["k0", "krem", "q", "k1", "gram", "v0", "v1", "v2",
             "txt", "v3", "v4", "pT", "semq0", "semq1", "s0", "s1"])}
        act_job = {n: i + 1 for i, n in enumerate(
            ["k0_32", "k0_hi", "krem_32", "krem_hi", "q_32", "q_hi", "k1_hi", "gram", "v0", "v1", "v2",
             "e0", "e1", "v3", "v4", "pT", "s0_hi", "s1_hi"])}
        dve_job = {n: i + 1 for i, n in enumerate(
            ["k0_r", "krem_r", "q_r", "k1_r", "max", "nmax", "rsum", "p0", "p1", "semq0", "semq1",
             "s0_r", "s1_r"])}

        block = ctx.enter_context(nc.Block())

        def passes(item):
            def run(eng):
                for layer in range(LAYERS):
                    n0 = layer * B
                    item(n0, layer)
                    with eng.Fori(n0 + 1, n0 + B - 1) as n:
                        item(n, layer)
                    item(n0 + B - 1, layer)
            return run

        def q1_here(n, layer):
            return (layer == 0 and not (isinstance(n, int) and n == 0)) or (isinstance(n, int) and n == B)

        def y_here(n):
            return not (isinstance(n, int) and n == 0)

        @block.sync
        def _(sp):
            for s in dma_signals:
                s.start(sp)

            def const(dst, src):
                sp.dma_start(dst, src).then_inc(consts_in, 16)

            const(wkt[:, :, :], wk_text.rearrange("(a p) c -> p a c", p=P))
            const(wki[:, :, :], wk_ip.rearrange("(a p) c -> p a c", p=P))
            for layer in range(LAYERS):
                const(wq_sb[:, layer, 0, :], wq[layer, 0:P, :])
                const(wq_sb[0:CT, layer, 1, :], wq[layer, P:C, :])
            const(wvt[:, :, :], wv_text.rearrange("(a p) c -> p a c", p=P))
            const(wvi[:, :, :], wv_ip.rearrange("(a p) c -> p a c", p=P))
            const(id_f[:, :], ident)
            const(den_sb[:, :], den_of)
            const(rows_sb[:, :], first_rows)
            for layer in range(LAYERS):
                const(wo_sb[:, layer, :, :], wo[layer])
                const(bo_sb[:, layer, 0:1], bo[layer, 0:P].rearrange("(p a) -> p a", a=1))
                const(bo_sb[0:CT, layer, 1:2], bo[layer, P:C].rearrange("(p a) -> p a", a=1))
            sp.wait_ge(init_done, 4)
            for j in range(HG):
                const(mask_sb[VW * j + IPC:VW * j + IPC + D, :],
                      mask.rearrange("(a s) -> a s", a=1).broadcast_to((D, S)))
            for g in range(NG):
                for j in range(HG):
                    sp.dma_start(ks[MROW:KROWS, g, j, :], key_kind).then_inc(kinds_in, 16)
                    sp.dma_start(vtile[:, g, :, j, :], value_ones).then_inc(kinds_in, 16)

            def load_batch(b):
                sp.dma_start(ctx_sb[:, 0, :], ctxT[b, 0:P, :]).then_inc(ctx_in.sem, 16)
                sp.dma_start(ctx_sb[:, 1, :], ctxT[b, P:CD, :]).then_inc(ctx_in.sem, 16)
                sp.dma_start(x_sb[:, 0, :], xT[b, 0:P, :]).then_inc(x_in.sem, 16)
                sp.dma_start(x_sb[0:CT, 1, :], xT[b, P:C, :]).then_inc(x_in.sem, 16)

            def store_batch(b, load_next):
                for u, name in enumerate(UNITS):
                    if name == "s0":
                        if load_next:
                            sp.wait_ge(products.sem, products.at(b, pe_job["v4"]))
                            load_batch(b + 1)
                        sp.wait_ge(dve_prep.sem, dve_prep.at(b, dve_job["semq1"]))
                        sp.dma_start(sem_q_dram[b], sem_q[:, :, :]).then_inc(sem_q_stored.sem, 16)
                    sp.wait_ge(split_done.sem, split_done.at(b, 2 * u + 2))
                    done = unit_stored[u].sem
                    src = parts[u]
                    if name in ("s0", "s1"):
                        h = int(name[1])
                        sp.dma_start(sem_k_dram[b, :, :, h * L:(h + 1) * L], src).then_inc(done, 16)
                        continue
                    for r in range(PARTS):
                        if name in ("k0", "k1"):
                            dst = k_stack[int(name[1]), b, r, :, 0:P, :]
                            sp.dma_start(dst.rearrange("i c k -> c i k"), src).then_inc(done, 16)
                        elif name == "krem":
                            for layer in range(LAYERS):
                                dst = k_stack[layer, b, r, :, P:C, :]
                                sp.dma_start(dst.rearrange("i c k -> c i k"),
                                             src[layer * CT:(layer + 1) * CT]).then_inc(done, 16)
                        else:
                            dst = q_stack[0, b, :, r, 0:P, :]
                            sp.dma_start(dst.rearrange("j c k -> c j k"), src[:, :, 0:S]).then_inc(done, 16)
                            dst = q_stack[0, b, :, r, P:C, :]
                            sp.dma_start(dst.rearrange("j c k -> c j k"), src[0:CT, :, S:2 * S]).then_inc(done, 16)

            load_batch(0)
            with sp.Fori(0, B - 1) as b:
                store_batch(b, True)
            store_batch(B - 1, False)

            for s in (*unit_stored, sem_q_stored):
                sp.wait_ge(s.sem, s.at(B - 1, s.per))
            sp.wait_ge(kinds_in, 2 * H * 16)

            def load_kq(layer, b, g):
                sp.dma_start(ks[0:STACK, g, :, :], k_stack[layer, b].rearrange(
                    "j i (d h) k -> (j i d) h k", d=D)[:, HG * g:HG * g + HG, :]).then_inc(kq_in[g].sem, 16)
                sp.dma_start(qs[0:STACK, g, :, :], q_stack[layer, b].rearrange(
                    "j i (d h) k -> (j i d) h k", d=D)[:, HG * g:HG * g + HG, :]).then_inc(kq_in[g].sem, 16)

            def load_sem_q(n, b):
                sp.dma_start(sem_q[:, :, :], sem_q_dram[b]).then_inc(sem_q_in.sem, 16)

            def m_rows(n, g):
                sp.wait_ge(m_row_out.sem, m_row_out.at(n, g + 1))
                for j in range(HG):
                    sp.dma_start(qs[MROW:KROWS, g, j, :], mrow[j:MR * HG:HG, :]).then_inc(m_row_in.sem, 16)

            for g in range(NG):
                if g == 0:
                    load_sem_q(0, 0)
                load_kq(0, 0, g)
            m_rows(0, 0)

            def item(n, layer):
                b = n - layer * B
                edge = isinstance(n, int)
                last_of_layer = edge and b == B - 1
                nxt = None if edge and n == ITEMS - 1 else ((1, 0) if last_of_layer else (layer, b + 1))
                for g in range(NG):
                    if g == 0 and layer == 0:
                        sp.wait_ge(s_ready.sem, s_ready.at(n, 0))
                        sp.dma_start(sem_k[:, :, :], sem_k_dram[b]).then_inc(sem_k_in.sem, 16)
                    if g >= 1 and nxt is not None:
                        sp.wait_ge(s_ready.sem, s_ready.at(n, HG * g))
                        if g == 1 and nxt[0] == 1:
                            sp.wait_ge(q1_stored.sem, q1_stored.at(nxt[1], 6))
                        load_kq(*nxt, g - 1)
                    elif g == 0 and not (edge and n == 0):
                        sp.wait_ge(s_ready.sem, s_ready.at(n, 0))
                        load_kq(layer, b, NG - 1)
                    if g == 1 and y_here(n):
                        store_y(n - 1, 0 if edge and n == B else layer)
                    if g == 2:
                        sp.wait_ge(y_ready.sem, y_ready.at(n, 0))
                        if layer == 1:
                            sp.wait_ge(y_stored.sem, y_stored.at(b, 2))
                        src = xT if layer == 0 else x1_dram
                        sp.dma_start(res[:, 0, :], src[b, 0:P, :]).then_inc(res_in.sem, 16)
                        sp.dma_start(res[0:CT, 1, :], src[b, P:C, :]).then_inc(res_in.sem, 16)
                    if g == 3 and layer == 0 and not last_of_layer:
                        sp.wait_ge(a_taken.sem, a_taken.at(n, 2 * H))
                        load_sem_q(n + 1, b + 1)
                    if g == 3 and q1_here(n, layer):
                        sp.wait_ge(q1_split.sem, q1_split.at(n - 1, 2))
                        for r in range(PARTS):
                            sp.dma_start(q_stack[1, n - 1, :, r, 0:P, :].rearrange("j c k -> c j k"),
                                         q_parts[:, :, 0:S]).then_inc(q1_stored.sem, 16)
                            sp.dma_start(q_stack[1, n - 1, :, r, P:C, :].rearrange("j c k -> c j k"),
                                         q_parts[0:CT, :, S:2 * S]).then_inc(q1_stored.sem, 16)
                    if g < NG - 1:
                        m_rows(n, g + 1)
                    elif nxt is not None:
                        m_rows(n + 1, 0)

            def store_y(n, layer):
                sp.wait_ge(y_ready.sem, y_ready.at(n, 2))
                dst = (x1_dram if layer == 0 else out)[n - layer * B]
                sp.dma_start(dst[0:P, :], y_sb[:, 0, :]).then_inc(y_stored.sem, 16)
                sp.dma_start(dst[P:C, :], y_sb[0:CT, 1, :]).then_inc(y_stored.sem, 16)

            passes(item)(sp)
            store_y(ITEMS - 1, 1)
            sp.wait_ge(y_stored.sem, y_stored.at(ITEMS - 1, 2))

        @block.gpsimd
        def _(pool):
            for s in pool_signals:
                s.start(pool)
            pool.memset(mask_sb[:, :], 1.0).then_inc(init_done, 1)
            pool.memset(ks[:, :, :, :], 0.0).then_inc(init_done, 1)
            pool.memset(qs[:, :, :, :], 0.0).then_inc(init_done, 1)
            pool.memset(gram[:, 0:T], 0.0).then_inc(init_done, 1)
            with pool.Fori(0, B) as b:
                for u, name in enumerate(UNITS):
                    pool.wait_ge(dve_prep.sem, dve_prep.at(b, dve_job[name + "_r"]))
                    pool.wait_ge(unit_stored[u].sem, unit_stored[u].at(b, 0))
                    pool.sem_inc(waited_pool, 1)
                    pool.tensor_copy(parts[u][:, 1, :], rest[u]).then_inc(split_done.sem, 1)
                    pool.wait_ge(split_done.sem, split_done.at(b, 2 * u + 1))
                    pool.tensor_tensor(parts[u][:, 2, :], rest[u], parts[u][:, 1, :],
                                       ALU.subtract).then_inc(split_done.sem, 1)

            def place_values(n, layer, b, g):
                cols = slice(HG * D * g, HG * D * (g + 1))

                def v(k0, k1):
                    return vals[:, layer, bass.ds(b, 1), k0:k1, cols].rearrange(
                        "p a k (h d) -> p (a k) h d", h=HG)
                pool.sem_inc(waited_pool, 1)
                pool.tensor_copy(vtile[:, g, 0:1, :, 0:D], v(0, 1))
                pool.tensor_copy(vtile[:, g, :, :, IPC:IPC + D], v(1, KC + 1)).then_inc(v_placed.sem, 1)

            def split_max(n, g):
                pool.wait_ge(a_taken.sem, a_taken.at(n, 2 * HG * (g + 1)))
                pool.wait_ge(m_turned.sem, m_turned.at(n, g))
                pool.sem_inc(waited_pool, 1)
                s = m_split.sem
                at = 4 * g

                def part(i):
                    return mpart[:, :, :, i, :]
                mxg = mx[:, g, :, :, :]
                r1 = mres[:, :, :, :]
                pool.tensor_copy(part(0), mxg).then_inc(s, 1)
                pool.wait_ge(m_split.sem, m_split.at(n, at + 1))
                pool.tensor_tensor(r1, mxg, part(0), ALU.subtract).then_inc(s, 1)
                pool.wait_ge(m_split.sem, m_split.at(n, at + 2))
                pool.sem_inc(waited_pool, 1)
                pool.tensor_copy(part(1), r1).then_inc(s, 1)
                pool.wait_ge(m_split.sem, m_split.at(n, at + 3))
                pool.tensor_tensor(part(2), r1, part(1), ALU.subtract).then_inc(s, 1)

            def normalise(n, layer, g):
                pool.wait_ge(inv_ready.sem, inv_ready.at(n, g + 1))
                pool.wait_ge(y_mm.sem, y_mm.at(n, 0))
                pool.tensor_tensor(hs[:, g, :], pv_sb[:, :], inv[:, :], ALU.mult)\
                    .then_inc((hs_unmasked if layer == 0 else hs_ready).sem, 1)
                if layer == 0:
                    pool.wait_ge(hs_unmasked.sem, hs_unmasked.at(n, g + 1))
                    pool.wait_ge(consts_in, N_CONST * 16)
                    pool.tensor_tensor(hs[:, g, :], hs[:, g, :], mask_sb[:, :], ALU.mult)\
                        .then_inc(hs_ready.sem, 1)

            for s in (act_prep,):
                pool.wait_ge(s.sem, s.at(B - 1, act_job["s1_hi"]))
            pool.wait_ge(kinds_in, 2 * H * 16)
            for g in range(NG - 1):
                place_values(0, 0, 0, g)
            split_max(0, 0)

            def item(n, layer):
                b = n - layer * B
                edge = isinstance(n, int)
                last_of_layer = edge and b == B - 1
                nxt = None if edge and n == ITEMS - 1 else ((1, 0) if last_of_layer else (layer, b + 1))
                for g in range(NG):
                    if g < NG - 1:
                        split_max(n, g + 1)
                    elif nxt is not None:
                        split_max(n + 1, 0)
                    if g == 0:
                        if not (edge and n == 0):
                            pool.wait_ge(pv_ready.sem, pv_ready.at(n, 0))
                        place_values(n, layer, b, NG - 1)
                    if g >= 2 and nxt is not None:
                        pool.wait_ge(pv_ready.sem, pv_ready.at(n, g - 1))
                        place_values(n + 1, *nxt, g - 2)
                    if g == NG - 1 and nxt is not None:
                        pool.wait_ge(pv_ready.sem, pv_ready.at(n, NG - 1))
                        place_values(n + 1, *nxt, NG - 2)
                    if g > 0:
                        normalise(n, layer, g - 1)
                    elif not (edge and n == 0):
                        normalise(n - 1, 0 if edge and n == B else layer, NG - 1)
                    if g == 1 and q1_here(n, layer):
                        pool.wait_ge(q1_rest.sem, q1_rest.at(n - 1, 1))
                        pool.wait_ge(q1_stored.sem, q1_stored.at(n - 1, 0))
                        pool.sem_inc(waited_pool, 1)
                        pool.tensor_copy(q_parts[:, 1, :], q_rest[:, :]).then_inc(q1_split.sem, 1)
                        pool.wait_ge(q1_split.sem, q1_split.at(n - 1, 1))
                        pool.tensor_tensor(q_parts[:, 2, :], q_rest[:, :], q_parts[:, 1, :],
                                           ALU.subtract).then_inc(q1_split.sem, 1)

            passes(item)(pool)
            normalise(ITEMS - 1, 1, NG - 1)

        @block.tensor
        def _(pe):
            for s in pe_signals:
                s.start(pe)
            pe.wait_ge(consts_in, N_CONST * 16)

            def free_bank(b, name):
                last = {"k0": ("a", "e1", 0), "krem": ("a", "v3", 0), "q": ("a", "v4", 0), "k1": ("a", "pT", 0),
                        "gram": ("d", "semq0", 0), "v0": ("d", "semq1", 0), "v1": ("d", "s0_r", 0),
                        "v2": ("d", "s1_r", 0), "txt": ("d", "k0_r", 1), "v3": ("d", "krem_r", 1),
                        "v4": ("d", "q_r", 1), "pT": ("d", "k1_r", 1), "semq0": ("a", "gram", 1),
                        "semq1": ("a", "v0", 1), "s0": ("a", "v1", 1), "s1": ("a", "v2", 1)}[name]
                sig, jobs = (act_prep, act_job) if last[0] == "a" else (dve_prep, dve_job)
                pe.wait_ge(sig.sem, sig.at(b, jobs[last[1]] - (0 if last[2] else sig.per)))

            def done(mm):
                mm.then_inc(products.sem, 1)

            with pe.Fori(0, B) as b:
                def keys(name, cols):
                    o = pbank[(pe_job[name] - 1) % 8]
                    free_bank(b, name)
                    for w, ks_ in ((wkt, slice(0, T)), (wki, slice(T, L))):
                        for a in range(2):
                            mm = pe.matmul(o[:, ks_], w[:, a, cols], ctx_sb[:, a, ks_],
                                           start=(a == 0), stop=(a == 1))
                    done(mm)

                def values(i):
                    name = f"v{i}"
                    o = pbank[(pe_job[name] - 1) % 8][:, 0:LAYERS * C]
                    free_bank(b, name)
                    w = wvt if i == 0 else wvi
                    c = max(i - 1, 0)
                    for a in range(2):
                        mm = pe.matmul(o, ctx_sb[:, a, c * P:(c + 1) * P], w[:, a, :],
                                       start=(a == 0), stop=(a == 1))
                    done(mm)

                pe.wait_ge(ctx_in.sem, ctx_in.at(b, 2))
                keys("k0", slice(0, P))
                keys("krem", slice(2 * P, 3 * P))
                free_bank(b, "q")
                pe.wait_ge(x_in.sem, x_in.at(b, 2))
                o = pbank[2].rearrange("p (a s) -> p a s", a=2)
                for m in range(2):
                    pe.matmul(o[:, m, :], wq_sb[:, 0, 0, m * P:(m + 1) * P], x_sb[:, 0, :], start=True, stop=False)
                    mm = pe.matmul(o[:, m, :], wq_sb[0:CT, 0, 1, m * P:(m + 1) * P], x_sb[0:CT, 1, :],
                                   start=False, stop=True)
                done(mm)
                keys("k1", slice(P, 2 * P))
                free_bank(b, "gram")
                for a in range(2):
                    mm = pe.matmul(pbank[4][0:T, T:L], ctx_sb[:, a, 0:T], ctx_sb[:, a, T:L],
                                   start=(a == 0), stop=(a == 1))
                done(mm)
                for i in range(3):
                    values(i)
                free_bank(b, "txt")
                pe.wait_ge(act_prep.sem, act_prep.at(b, act_job["q_32"]))
                for t in range(QT):
                    pe.matmul(pbank[0][:, t * T:(t + 1) * T], qt32[:, 0, t * P:(t + 1) * P], kt32[:, 0, :],
                              start=True, stop=False)
                    mm = pe.matmul(pbank[0][:, t * T:(t + 1) * T], qt32[0:CT, 1, t * P:(t + 1) * P],
                                   kt32[0:CT, 1, :], start=False, stop=True)
                done(mm)
                values(3)
                values(4)
                free_bank(b, "pT")
                pe.wait_ge(dve_prep.sem, dve_prep.at(b, dve_job["p1"]))
                for t in range(QT):
                    mm = pe.transpose(pbank[3][0:T, t * P:(t + 1) * P], p_txt[:, t, :], id_f[:, :])
                done(mm)
                pe.wait_ge(act_prep.sem, act_prep.at(b, act_job["pT"]))
                for t in range(QT):
                    free_bank(b, f"semq{t}")
                    done(pe.matmul(pbank[4 + t][:, 0:L - T], pT_txt[:, t * P:(t + 1) * P], gram[:, T:L],
                                   start=True, stop=True))
                for h in range(2):
                    free_bank(b, f"s{h}")
                    for c in range(2):
                        k = 2 * h + c
                        mm = pe.matmul(pbank[6 + h][:, c * S:(c + 1) * S], gram[:, k * P:(k + 1) * P],
                                       pT_txt[:, :], start=True, stop=True)
                    done(mm)

            pe.wait_ge(dve_prep.sem, dve_prep.at(B - 1, dve_prep.per))
            pe.wait_ge(act_prep.sem, act_prep.at(B - 1, act_prep.per))

            pe.wait_ge(id_b_ready, 1)

            def by_query(n, g, j):
                if j == 0:
                    pe.wait_ge(kq_in[g].sem, kq_in[g].at(n, 2))
                for t in range(QT):
                    i = 2 * HG * g + 2 * j + t
                    pe.wait_ge(a_taken.sem, a_taken.at(n, i - 1))
                    pe.matmul(bank[t][:, :], qs[0:MROW, g, j, t * P:(t + 1) * P], ks[0:MROW, g, j, :],
                              start=True, stop=True).then_inc(a_ready.sem, 1)

            def by_key(n, layer, g, j):
                h = HG * g + j
                o = sc[j % 2]
                if j == 0:
                    pe.wait_ge(m_row_in.sem, m_row_in.at(n, HG * (g + 1)))
                    if g == 0 and layer == 0:
                        pe.wait_ge(sem_k_in.sem, sem_k_in.at(n, 1))
                pe.wait_ge(probs_ready.sem, probs_ready.at(n, h - 1))
                for half_ in range(2):
                    for c in range(2):
                        k = 2 * half_ + c
                        mm = pe.matmul(o[:, half_, c * S:(c + 1) * S], ks[0:KROWS, g, j, k * P:(k + 1) * P],
                                       qs[0:KROWS, g, j, :], start=(layer == 1 or c == 0), stop=(layer == 1),
                                       skip_group_check=(layer == 0))
                    if layer == 0:
                        for i in range(PARTS):
                            mm = pe.matmul(o[:, half_, :], id_b[:, :], sem_k[:, i, half_ * L:(half_ + 1) * L],
                                           start=False, stop=(i == PARTS - 1), skip_group_check=True)
                mm.then_inc(s_ready.sem, 1)

            def times_values(n, g):
                pe.wait_ge(probs_ready.sem, probs_ready.at(n, HG * (g + 1)))
                pe.wait_ge(inv_ready.sem, inv_ready.at(n, g))
                pe.wait_ge(v_placed.sem, v_placed.at(n, g + 1))
                for c in range(KC):
                    for j in range(HG):
                        mm = pe.matmul(pv_bank[VW * j:VW * (j + 1), 0:S], vtile[:, g, c, j, :],
                                       probs[:, (HG * g + j) % RING, c * S:(c + 1) * S],
                                       start=(c == 0), stop=(c == KC - 1))
                mm.then_inc(pv_ready.sem, 1)

            def denominators(n, g):
                pe.wait_ge(pv_copied.sem, pv_copied.at(n, g + 1))
                pe.matmul(pv_bank[:, S:2 * S], den_sb[:, :], pv_sb[:, :], start=True, stop=True)\
                    .then_inc(den_ready.sem, 1)

            def turn_max(n, g, after=None):
                pe.wait_ge(m_split.sem, m_split.at(n, 4 * (g + 1)))
                pe.wait_ge(m_row_out.sem, m_row_out.at(n, g))
                for t in range(QT):
                    mm = pe.transpose(misc[0:MR * HG, :].bitcast(BF16)[:, t * P:(t + 1) * P],
                                      mpart[:, t, :, :, :].rearrange("p a b c -> p (a b c)"), id_b[:, :])
                mm.then_inc(m_turned.sem, 1)

            def project_out(n, layer):
                pe.wait_ge(hs_ready.sem, hs_ready.at(n, NG))
                pe.wait_ge(m_row_out.sem, m_row_out.at(n + 1, 2))
                for m, (c0, c1) in enumerate(((0, P), (P, C))):
                    for g in range(NG):
                        mm = pe.matmul(misc[0:c1 - c0, m * S:(m + 1) * S], wo_sb[:, layer, g, c0:c1],
                                       hs[:, g, :], start=(g == 0), stop=(g == NG - 1))
                mm.then_inc(y_mm.sem, 1)

            def project_q1(n):
                pe.wait_ge(y_ready.sem, y_ready.at(n, 2))
                pe.wait_ge(m_row_out.sem, m_row_out.at(n + 1, 3))
                for m in range(2):
                    o = misc[:, m * S:(m + 1) * S]
                    pe.matmul(o, wq_sb[:, 1, 0, m * P:(m + 1) * P], y_sb[:, 0, :], start=True, stop=False)
                    mm = pe.matmul(o, wq_sb[0:CT, 1, 1, m * P:(m + 1) * P], y_sb[0:CT, 1, :],
                                   start=False, stop=True)
                mm.then_inc(q1_mm.sem, 1)

            for g in range(2):
                for j in range(HG):
                    by_query(0, g, j)
            turn_max(0, 0)

            def item(n, layer):
                b = n - layer * B
                edge = isinstance(n, int)
                final = edge and n == ITEMS - 1
                for g in range(NG):
                    ahead = (n, g + 2) if g + 2 < NG else (None if final else (n + 1, g + 2 - NG))
                    before = (n, g - 1) if g > 0 else (None if edge and n == 0 else (n - 1, NG - 1))

                    def a(j):
                        if ahead is not None:
                            by_query(*ahead, j)
                    if g == 0:
                        a(0)
                        a(1)
                        if before:
                            times_values(*before)
                        by_key(n, layer, g, 0)
                        by_key(n, layer, g, 1)
                    else:
                        by_key(n, layer, g, 0)
                        a(0)
                        by_key(n, layer, g, 1)
                        a(1)
                        times_values(*before)
                    if g < NG - 1:
                        if g == 1 and y_here(n):
                            pe.wait_ge(y_ready.sem, y_ready.at(n - 1, 2))
                        if g == 2 and q1_here(n, layer):
                            pe.wait_ge(q1_rest.sem, q1_rest.at(n - 1, 1))
                        turn_max(n, g + 1)
                    elif not final:
                        turn_max(n + 1, 0)
                    by_key(n, layer, g, 2)
                    a(2)
                    if before:
                        denominators(*before)
                    by_key(n, layer, g, 3)
                    a(3)
                    if g == 0 and y_here(n):
                        project_out(n - 1, 0 if edge and n == B else layer)
                    if g == 1 and q1_here(n, layer):
                        project_q1(n - 1)

            passes(item)(pe)
            n = ITEMS - 1
            times_values(n, NG - 1)
            denominators(n, NG - 1)
            pe.wait_ge(hs_ready.sem, hs_ready.at(n, NG))
            for m, (c0, c1) in enumerate(((0, P), (P, C))):
                for g in range(NG):
                    mm = pe.matmul(misc[0:c1 - c0, m * S:(m + 1) * S], wo_sb[:, 1, g, c0:c1],
                                   hs[:, g, :], start=(g == 0), stop=(g == NG - 1))
            mm.then_inc(y_mm.sem, 1)

        @block.scalar
        def _(act):
            for s in act_signals:
                s.start(act)
            act.wait_ge(consts_in, N_CONST * 16)
            act.activation(id_b[:, :], id_f[:, :], ACT.Copy).then_inc(id_b_ready, 1)

            with act.Fori(0, B) as b:
                def bank_of(name):
                    return pbank[(pe_job[name] - 1) % 8]

                def copy(name, dst, src, **kw):
                    return act.activation(dst, src, kw.pop("func", ACT.Copy), **kw).then_inc(act_prep.sem, 1)

                def high_part(u):
                    act.wait_ge(unit_stored[u].sem, unit_stored[u].at(b, 0))
                    copy("hi", parts[u][:, 0, :], bank_of(UNITS[u]))

                def values(i):
                    act.wait_ge(products.sem, products.at(b, pe_job[f"v{i}"]))
                    keep = {"scale": rows_sb[:, i:i + 1]} if i < 2 else {}
                    copy("v", vals[:, :, bass.ds(b, 1), i, :].rearrange("p l a c -> p (l a) c"),
                         bank_of(f"v{i}")[:, 0:LAYERS * C].rearrange("p (l c) -> p l c", l=LAYERS), **keep)

                act.wait_ge(products.sem, products.at(b, pe_job["k0"]))
                copy("k32", kt32[:, 0, :], bank_of("k0")[:, 0:T])
                high_part(0)
                act.wait_ge(products.sem, products.at(b, pe_job["krem"]))
                copy("k32", kt32[0:CT, 1, :], bank_of("krem")[0:CT, 0:T])
                high_part(1)
                act.wait_ge(products.sem, products.at(b, pe_job["q"]))
                copy("q32", qt32[:, :, :].rearrange("p a s -> p (a s)"), bank_of("q"))
                high_part(2)
                act.wait_ge(products.sem, products.at(b, pe_job["k1"]))
                high_part(3)
                act.wait_ge(products.sem, products.at(b, pe_job["gram"]))
                copy("gram", gram[:, T:L], bank_of("gram")[0:T, T:L], scale=SEM_SCALE)
                for i in range(3):
                    values(i)
                act.wait_ge(dve_prep.sem, dve_prep.at(b, dve_job["nmax"]))
                for t in range(QT):
                    copy("e", e_txt[:, t, :], bank_of("txt")[:, t * T:(t + 1) * T], func=ACT.Exp,
                         bias=stat[:, 1, t:t + 1], scale=SCALE, accum_out=stat[:, 2, t:t + 1])
                for i in range(3, 5):
                    values(i)
                act.wait_ge(products.sem, products.at(b, pe_job["pT"]))
                copy("pT", pT_txt[:, :], bank_of("pT")[0:T, 0:S])
                for h in range(2):
                    act.wait_ge(products.sem, products.at(b, pe_job[f"s{h}"]))
                    high_part(4 + h)

            for s in unit_stored:
                act.wait_ge(s.sem, s.at(B - 1, s.per))
            act.wait_ge(split_done.sem, split_done.at(B - 1, split_done.per))

            def exponentials(n, g, j):
                h = HG * g + j
                act.wait_ge(s_ready.sem, s_ready.at(n, h + 1))
                act.wait_ge(pv_ready.sem, pv_ready.at(n, (h - RING) // HG + 1))
                act.activation(probs[:, h % RING, :], sc[j % 2][:, :, :].rearrange("p a b -> p (a b)"),
                               ACT.Exp, scale=SCALE).then_inc(probs_ready.sem, 1)

            def take_m_rows(n, g):
                act.wait_ge(m_turned.sem, m_turned.at(n, g + 1))
                act.wait_ge(m_row_in.sem, m_row_in.at(n, HG * g))
                act.activation(mrow[:, :], misc[0:MR * HG, :].bitcast(BF16)[:, 0:S], ACT.Copy)\
                    .then_inc(m_row_out.sem, 1)

            def copy_pv(n, g):
                act.wait_ge(pv_ready.sem, pv_ready.at(n, g + 1))
                act.wait_ge(hs_ready.sem, hs_ready.at(n, g))
                act.activation(pv_sb[:, :], pv_bank[:, 0:S], ACT.Copy).then_inc(pv_copied.sem, 1)

            take_m_rows(0, 0)

            def item(n, layer):
                edge = isinstance(n, int)
                for g in range(NG):
                    exponentials(n, g, 0)
                    exponentials(n, g, 1)
                    if g > 0:
                        copy_pv(n, g - 1)
                    elif not (edge and n == 0):
                        copy_pv(n - 1, NG - 1)
                    if g < NG - 1:
                        take_m_rows(n, g + 1)
                    elif not (edge and n == ITEMS - 1):
                        take_m_rows(n + 1, 0)
                    exponentials(n, g, 2)
                    exponentials(n, g, 3)
                    if g == 1 and q1_here(n, layer):
                        act.wait_ge(q1_mm.sem, q1_mm.at(n - 1, 1))
                        act.wait_ge(q1_stored.sem, q1_stored.at(n - 1, 0))
                        act.activation(q_parts[:, 0, :], misc[:, :], ACT.Copy).then_inc(q1_hi.sem, 1)

            passes(item)(act)
            copy_pv(ITEMS - 1, NG - 1)

        @block.vector
        def _(dve):
            for s in dve_signals:
                s.start(dve)
            dve.wait_ge(consts_in, N_CONST * 16)
            with dve.Fori(0, B) as b:
                def bank_of(name):
                    return pbank[(pe_job[name] - 1) % 8]

                def take_rest(u):
                    name = UNITS[u]
                    dve.wait_ge(act_prep.sem, act_prep.at(b, act_job[name + "_hi"]))
                    dve.wait_ge(split_done.sem, split_done.at(b, 2 * u + 2 - split_done.per))
                    dve.tensor_tensor(rest[u], bank_of(name), parts[u][:, 0, :], ALU.subtract)\
                        .then_inc(dve_prep.sem, 1)

                for u in range(4):
                    take_rest(u)
                dve.wait_ge(products.sem, products.at(b, pe_job["txt"]))
                dve.tensor_reduce(stat[:, 0, :], bank_of("txt")[:, 0:QT * T].rearrange("p (t k) -> p t k", t=QT),
                                  AX, ALU.max).then_inc(dve_prep.sem, 1)
                dve.wait_ge(dve_prep.sem, dve_prep.at(b, dve_job["max"]))
                dve.tensor_scalar(stat[:, 1, :], stat[:, 0, :], -SCALE, None, ALU.mult).then_inc(dve_prep.sem, 1)
                dve.wait_ge(act_prep.sem, act_prep.at(b, act_job["e1"]))
                dve.reciprocal(stat[:, 3, :], stat[:, 2, :]).then_inc(dve_prep.sem, 1)
                dve.wait_ge(dve_prep.sem, dve_prep.at(b, dve_job["rsum"]))
                for t in range(QT):
                    dve.tensor_scalar(p_txt[:, t, :], e_txt[:, t, :], stat[:, 3, t:t + 1], None, ALU.mult)\
                        .then_inc(dve_prep.sem, 1)
                dve.wait_ge(sem_q_stored.sem, sem_q_stored.at(b, 0))
                for t in range(QT):
                    dve.wait_ge(products.sem, products.at(b, pe_job[f"semq{t}"]))
                    dve.tensor_copy(sem_q[:, t, :], bank_of(f"semq{t}")[:, 0:L - T]).then_inc(dve_prep.sem, 1)
                for u in range(4, 6):
                    take_rest(u)

            def maxima(n, layer, g, j):
                if layer == 0 and g == 0 and j == 0:
                    dve.wait_ge(sem_q_in.sem, sem_q_in.at(n, 1))
                for t in range(QT):
                    i = 2 * HG * g + 2 * j + t
                    dve.wait_ge(a_ready.sem, a_ready.at(n, i + 1))
                    dve.tensor_reduce(mx[:, g, t, 0, j:j + 1], bank[t][:, 0:T], AX, ALU.max)
                    if layer == 0:
                        dve.wait_ge(a_taken.sem, a_taken.at(n, i + 1 - FUSED))
                        dve.sem_inc(waited_dve, 1)
                        dve.tensor_tensor_reduce(fused[:, i % FUSED, :], bank[t][:, T:L], sem_q[:, t, :], 1.0,
                                                 -3.0e38, ALU.add, ALU.max, mx[:, g, t, 1, j:j + 1])\
                            .then_inc(a_taken.sem, 1)
                    else:
                        dve.tensor_reduce(mx[:, g, t, 1, j:j + 1], bank[t][:, T:L], AX, ALU.max)\
                            .then_inc(a_taken.sem, 1)

            def invert(n, g):
                dve.wait_ge(den_ready.sem, den_ready.at(n, g + 1))
                dve.wait_ge(hs_ready.sem, hs_ready.at(n, g))
                dve.reciprocal(inv[:, :], pv_bank[:, S:2 * S]).then_inc(inv_ready.sem, 1)

            def finish(n, layer):
                dve.wait_ge(y_mm.sem, y_mm.at(n, 1))
                dve.wait_ge(res_in.sem, res_in.at(n, 2))
                dve.wait_ge(y_stored.sem, y_stored.at(n, 0))
                for m, rows in enumerate((P, CT)):
                    dve.scalar_tensor_tensor(out=y_sb[0:rows, m, :], in0=misc[0:rows, m * S:(m + 1) * S],
                                             scalar=bo_sb[0:rows, layer, m:m + 1], in1=res[0:rows, m, :],
                                             op0=ALU.add, op1=ALU.add).then_inc(y_ready.sem, 1)

            for g in range(2):
                for j in range(HG):
                    maxima(0, 0, g, j)

            def item(n, layer):
                edge = isinstance(n, int)
                final = edge and n == ITEMS - 1
                next_layer = 1 if edge and n == B - 1 else layer
                for g in range(NG):
                    ahead = (n, layer, g + 2) if g + 2 < NG else (None if final else (n + 1, next_layer, g + 2 - NG))
                    for j in range(HG - 1):
                        if ahead is not None:
                            maxima(*ahead, j)
                    if g > 0:
                        invert(n, g - 1)
                    elif not (edge and n == 0):
                        invert(n - 1, NG - 1)
                    if ahead is not None:
                        maxima(*ahead, HG - 1)
                    if g == 0 and y_here(n):
                        finish(n - 1, 0 if edge and n == B else layer)
                    if g == 1 and q1_here(n, layer):
                        dve.wait_ge(q1_hi.sem, q1_hi.at(n - 1, 1))
                        dve.wait_ge(q1_split.sem, q1_split.at(n - 1, 0))
                        dve.tensor_tensor(q_rest[:, :], misc[:, :], q_parts[:, 0, :], ALU.subtract)\
                            .then_inc(q1_rest.sem, 1)

            passes(item)(dve)
            invert(ITEMS - 1, NG - 1)
            finish(ITEMS - 1, 1)


def kernel(x, ctx_2048, fside_S_0, L0_xattn_Wq, L0_xattn_Wk, L0_xattn_Wv, L0_xattn_Wk_ip, L0_xattn_Wv_ip,
           L0_xattn_Wout, L0_xattn_bout, L1_xattn_Wq, L1_xattn_Wk, L1_xattn_Wv, L1_xattn_Wk_ip,
           L1_xattn_Wv_ip, L1_xattn_Wo, L1_xattn_bo):
    import numpy as np
    import concourse.bacc as bacc
    from concourse.bass_utils import run_bass_kernel_spmd

    f = np.float32

    def dims_first(w):
        return np.asarray(w).reshape(w.shape[0], H, D).transpose(0, 2, 1).reshape(w.shape[0], C)

    def side_by_side(w0, w1):
        w0, w1 = dims_first(w0), dims_first(w1)
        pad = np.zeros((CD, 3 * P - 2 * C), f)
        return np.concatenate([w0[:, :P], w1[:, :P], w0[:, P:], w1[:, P:], pad], axis=1)

    def by_value_rows(w):
        rows = np.zeros((NG, HG, VW, C), f)
        w = np.asarray(w).reshape(NG, HG, D, C)
        rows[:, :, 0:D] = w
        rows[:, :, IPC:IPC + D] = w
        return rows.reshape(NG, P, C).transpose(1, 0, 2)

    wq = np.zeros((LAYERS, C, 2 * P), f)
    wq[0, :, :C] = dims_first(L0_xattn_Wq)
    wq[1, :, :C] = dims_first(np.asarray(L1_xattn_Wq).T)
    kind = np.zeros((MR, L), f)
    kind[:PARTS, :T] = -1
    kind[PARTS:, T:] = -1
    ones = np.zeros((P, KC, VW), f)
    ones[:T, 0, D] = 1
    ones[T:, 0, IPC + D] = 1
    ones[:, 1:, IPC + D] = 1
    den_of = np.zeros((P, P), f)
    for m in range(P):
        r = m % VW
        den_of[m - r + (IPC + D if IPC <= r <= IPC + D else D), m] = 1
    first_rows = np.zeros((P, 2), f)
    first_rows[:T, 0] = 1
    first_rows[T:, 1] = 1
    arrays = {
        "xT": np.asarray(x).transpose(0, 2, 1),
        "ctxT": np.asarray(ctx_2048).transpose(0, 2, 1),
        "mask": np.asarray(fside_S_0),
        "wk_text": side_by_side(L0_xattn_Wk, np.asarray(L1_xattn_Wk).T),
        "wk_ip": side_by_side(L0_xattn_Wk_ip, np.asarray(L1_xattn_Wk_ip).T),
        "wv_text": np.concatenate([np.asarray(L0_xattn_Wv), np.asarray(L1_xattn_Wv).T], axis=1),
        "wv_ip": np.concatenate([np.asarray(L0_xattn_Wv_ip), np.asarray(L1_xattn_Wv_ip).T], axis=1),
        "wq": wq,
        "wo": np.stack([by_value_rows(L0_xattn_Wout), by_value_rows(np.asarray(L1_xattn_Wo).T)]),
        "bo": np.stack([np.asarray(L0_xattn_bout), np.asarray(L1_xattn_bo)]),
        "ident": np.eye(P, dtype=f),
        "key_kind": kind.astype(mybir.dt.np(BF16)),
        "value_ones": ones,
        "den_of": den_of,
        "first_rows": first_rows,
    }
    arrays = {k: np.ascontiguousarray(v) for k, v in arrays.items()}
    nc = bacc.Bacc("TRN2", target_bir_lowering=False, num_devices=1)
    args = [nc.dram_tensor(k, v.shape, mybir.dt.from_np(v.dtype), kind="ExternalInput").ap()
            for k, v in arrays.items()]
    out = nc.dram_tensor("out", (B, C, S), F32, kind="ExternalOutput").ap()
    build(nc, *args, out)
    r = run_bass_kernel_spmd(nc, [arrays], core_ids=[0])
    return np.ascontiguousarray(r.results[0]["out"].transpose(0, 2, 1))
```

```python
from contextlib import ExitStack

import concourse.bass as bass
from concourse import mybir

F32 = mybir.dt.float32
BF16 = mybir.dt.bfloat16
ACT = mybir.ActivationFunctionType
ALU = mybir.AluOpType
AX = mybir.AxisListType.X

B, S, C, CD, L, T = 8, 256, 160, 256, 512, 77
H = 20
D = C // H
SCALE = float(D) ** -0.5
SEM_SCALE = 0.5
P = 128
LAYERS = 2
ITEMS = LAYERS * B
HG = 4
NG = H // HG
QT = S // P
KC = L // P
PARTS = 3
STACK = PARTS * PARTS * D
MROW = 96
MR = 2 * PARTS * HG
KROWS = MROW + MR
RING = 10
FUSED = 4
HALVES = 2 * HG
TURN = 3
ADDED = (0, 2, 4, 6, 7)
VW = 32
IPC = 9


class Signal:

    def __init__(self, sem, per, unit=1):
        self.sem, self.per, self.unit = sem, per, unit

    def start(self, eng):
        eng.sem_inc(self.sem, self.per * self.unit)

    def at(self, turn, count):
        return turn * (self.per * self.unit) + (self.per + count) * self.unit


def build(nc, xT, ctxT, mask, wk_text, wk_ip, wv_text, wv_ip, wq, wo, bo,
          ident, key_kind, value_ones, den_pick, first_rows, out):
    k_stack = nc.dram_tensor("k_stack", (LAYERS, B, PARTS, PARTS, D * H, L), BF16, kind="Internal").ap()
    q_stack = nc.dram_tensor("q_stack", (LAYERS, B, PARTS, PARTS, D * H, S), BF16, kind="Internal").ap()
    sem_q_dram = nc.dram_tensor("sem_q_dram", (B, P, QT, L - T), F32, kind="Internal").ap()
    sem_k_dram = nc.dram_tensor("sem_k_dram", (B, P, PARTS, KC * S), BF16, kind="Internal").ap()
    sem_k32_dram = nc.dram_tensor("sem_k32_dram", (B, P, KC * S), F32, kind="Internal").ap()
    x1_dram = nc.dram_tensor("x1_dram", (B, C, S), F32, kind="Internal").ap()
    CT = C - P

    with ExitStack() as ctx:
        def sb(name, shape, dt=F32):
            return ctx.enter_context(nc.sbuf_tensor(name, shape, dt))

        def sem(name):
            return ctx.enter_context(nc.semaphore(name))

        wk_sb = sb("wk_sb", [P, 2, 2, 3 * P])
        wv_sb = sb("wv_sb", [P, 2, 2, LAYERS * C])
        wkt, wki, wvt, wvi = wk_sb[:, 0], wk_sb[:, 1], wv_sb[:, 0], wv_sb[:, 1]
        wq_sb = sb("wq_sb", [P, LAYERS, 2, 2 * P])
        wo_sb = sb("wo_sb", [P, LAYERS, NG, C])
        bo_sb = sb("bo_sb", [P, LAYERS, 2])
        id_f = sb("id_f", [P, P])
        id_b = sb("id_b", [P, P], BF16)
        pick_sb = sb("pick_sb", [P, 2 * HG])
        rows_sb = sb("rows_sb", [P, 2])
        mask_sb = sb("mask_sb", [P, LAYERS, QT])
        ctx_sb = sb("ctx_sb", [P, 2, L])
        x_sb = sb("x_sb", [P, 2, S])
        kt32 = sb("kt32", [P, 2, T])
        qt32 = sb("qt32", [P, 2, S])
        gram = sb("gram", [T, L])
        e_txt = sb("e_txt", [P, QT, T])
        p_txt = sb("p_txt", [P, QT, T])
        pT_txt = sb("pT_txt", [T, S])
        stat = sb("stat", [P, 4, QT])
        ks = sb("ks", [P, NG, HG, L], BF16)
        qs = sb("qs", [P, NG, HG, S], BF16)
        vals = sb("vals", [P, LAYERS, B, KC + 1, C])
        vtile = sb("vtile", [P, NG, KC, HG, VW])
        probs = sb("probs", [P, RING, KC * S])
        sem_q_first = sb("sem_q", [P, QT, L - T])
        sem_k_first = sb("sem_k", [P, PARTS, KC * S], BF16)
        fused = sb("fused", [P, FUSED * (L - T)], BF16)
        mx = sb("mx", [P, NG, QT, 2, HG])
        mres = sb("mres", [P, QT, 2, HG])
        mpart = sb("mpart", [P, QT, 2, PARTS, HG], BF16)
        mrow = sb("mrow", [MR, S], BF16)
        inv = sb("inv", [P, QT, HG, 2])
        inv_wide = sb("inv_wide", [P, QT, HG, VW])
        sem_k32_first = sb("sem_k32", [P, KC * S])
        hs = sb("hs", [P, NG, S])
        res = sb("res", [P, 2, S])
        y_sb = sb("y_sb", [P, 2, S])
        q_parts = sb("q_parts", [P, PARTS, 2 * S], BF16)
        q_rest = sb("q_rest", [P, 2 * S])

        UNITS = ["k0", "krem", "q", "k1", "s0", "s1"]
        flat = probs[:, :, :].rearrange("p a b -> p (a b)")
        half = PARTS * L // 2
        parts = [flat[:, u * half:(u + 1) * half].bitcast(BF16).rearrange("p (a b) -> p a b", a=PARTS)
                 for u in range(6)]
        rest = [flat[:, 6 * half + u * L:6 * half + (u + 1) * L] for u in range(6)]

        sem_k32_out = flat[:, 6 * (half + L):6 * (half + L) + KC * S]
        sem_q_out = fused[:, :].bitcast(F32).rearrange("p (t k) -> p t k", t=QT)

        sem_q = [sem_q_first[:, :, :], ctx_sb[:, :, :].rearrange("p a b -> p (a b)")[:, 0:QT * (L - T)]
                 .rearrange("p (t k) -> p t k", t=QT)]
        sem_k = [sem_k_first[:, :, :], wk_sb[:, :, :, :].rearrange("p a b c -> p (a b c)").bitcast(BF16)
                 .rearrange("p (a b) -> p a b", a=PARTS)]
        sem_k32 = [sem_k32_first[:, :], wv_sb[:, :, :, :].rearrange("p a b c -> p (a b c)")[:, 0:KC * S]]

        by_query_bank = [ctx.enter_context(nc.psum_tensor(f"by_query{i}", [P, QT, 512], F32)) for i in range(2)]
        by_key_bank = [ctx.enter_context(nc.psum_tensor(f"by_key{i}", [P, 512], F32)) for i in range(2)]
        pv_bank = ctx.enter_context(nc.psum_tensor("pv_bank", [P, 512], F32))
        misc = ctx.enter_context(nc.psum_tensor("misc", [P, 512], F32))
        pbank = [by_query_bank[0][:, 0, :], by_query_bank[0][:, 1, :], by_query_bank[1][:, 0, :],
                 by_query_bank[1][:, 1, :], by_key_bank[0][:, :], by_key_bank[1][:, :], pv_bank[:, :], misc[:, :]]
        turned_max = by_key_bank[0][0:MR, 0:S // 2].bitcast(BF16)
        den = pv_bank[:, S:S + QT * 2 * HG]
        scale_rows = pv_bank[:, S:2 * S]

        keys_in = sem("keys_in")
        weights_in = sem("weights_in")
        zeroed = sem("zeroed")
        gram_zeroed = sem("gram_zeroed")
        pool_init = sem("pool_init")
        kinds_in = sem("kinds_in")
        id_b_ready = sem("id_b_ready")
        waited_pool = sem("waited_pool")
        waited_dve = sem("waited_dve")
        ctx_in = Signal(sem("ctx_in"), 2, 16)
        x_in = Signal(sem("x_in"), 2, 16)
        products = Signal(sem("products"), 16)
        act_prep = Signal(sem("act_prep"), 20)
        dve_prep = Signal(sem("dve_prep"), 13)
        split_done = Signal(sem("split_done"), 12)
        unit_stored = [Signal(sem(f"stored_{u}"), k, 16) for u, k in zip(UNITS, (3, 6, 6, 3, 1, 1))]
        sem_q_stored = Signal(sem("sem_q_stored"), 1, 16)
        sem_k32_stored = Signal(sem("sem_k32_stored"), 1, 16)
        prep_signals = [ctx_in, x_in, products, act_prep, dve_prep, split_done, sem_q_stored, sem_k32_stored, *unit_stored]
        kq_in = [Signal(sem(f"kq_in{g}"), 2, 16) for g in range(NG)]
        a_ready = Signal(sem("a_ready"), H)
        a_taken = Signal(sem("a_taken"), H)
        m_split = Signal(sem("m_split"), 4 * NG)
        m_turned = Signal(sem("m_turned"), NG)
        m_row_out = Signal(sem("m_row_out"), NG)
        m_row_in = Signal(sem("m_row_in"), NG, 16)
        s_ready = Signal(sem("s_ready"), HALVES * NG)
        probs_ready = Signal(sem("probs_ready"), HALVES * NG)
        v_placed = Signal(sem("v_placed"), NG)
        pv_ready = Signal(sem("pv_ready"), NG)
        pv_copied = Signal(sem("pv_copied"), NG)
        den_ready = Signal(sem("den_ready"), NG)
        inv_ready = Signal(sem("inv_ready"), NG)
        inv_widened = Signal(sem("inv_widened"), NG)
        scale_ready = Signal(sem("scale_ready"), NG)
        s_added = Signal(sem("s_added"), len(ADDED) * NG)
        hs_ready = Signal(sem("hs_ready"), NG)
        sem_q_in = Signal(sem("sem_q_in"), 1, 16)
        sem_k_in = Signal(sem("sem_k_in"), 2, 16)
        res_in = Signal(sem("res_in"), 2, 16)
        y_mm = Signal(sem("y_mm"), 1)
        y_ready = Signal(sem("y_ready"), 2)
        y_stored = Signal(sem("y_stored"), 2, 16)
        q1_mm = Signal(sem("q1_mm"), 1)
        q1_hi = Signal(sem("q1_hi"), 1)
        q1_rest = Signal(sem("q1_rest"), 1)
        q1_split = Signal(sem("q1_split"), 2)
        q1_stored = Signal(sem("q1_stored"), 6, 16)
        pe_signals = [a_ready, m_turned, s_ready, pv_ready, den_ready, scale_ready, y_mm, q1_mm, products]
        act_signals = [act_prep, m_row_out, probs_ready, pv_copied, q1_hi]
        dve_signals = [dve_prep, a_taken, s_added, inv_ready, hs_ready, y_ready, q1_rest]
        pool_signals = [split_done, m_split, v_placed, inv_widened, q1_split]
        dma_signals = [ctx_in, x_in, *unit_stored, sem_q_stored, sem_k32_stored, *kq_in, m_row_in, sem_q_in, sem_k_in,
                       res_in, y_stored, q1_stored]

        N_WEIGHTS = 6 + 5 * LAYERS
        pe_job = {n: i + 1 for i, n in enumerate(
            ["k0", "krem", "q", "k1", "gram", "v0", "v1", "v2",
             "txt", "v3", "v4", "pT", "semq0", "semq1", "s0", "s1"])}
        act_job = {n: i + 1 for i, n in enumerate(
            ["k0_32", "k0_hi", "krem_32", "krem_hi", "q_32", "q_hi", "k1_hi", "gram", "v0", "v1", "v2",
             "e0", "e1", "v3", "v4", "pT", "s0_32", "s0_hi", "s1_32", "s1_hi"])}
        dve_job = {n: i + 1 for i, n in enumerate(
            ["k0_r", "krem_r", "q_r", "k1_r", "max", "nmax", "rsum", "p0", "p1", "semq0", "semq1",
             "s0_r", "s1_r"])}

        block = ctx.enter_context(nc.Block())

        def passes(item):
            def run(eng):
                for layer in range(LAYERS):
                    n0 = layer * B
                    item(n0, layer, 0)
                    if layer == 0:
                        with eng.Fori(0, (B - 2) // 2) as pair:
                            item(pair * 2 + 1, layer, 1)
                            item(pair * 2 + 2, layer, 0)
                    else:
                        with eng.Fori(n0 + 1, n0 + B - 1) as n:
                            item(n, layer, 0)
                    item(n0 + B - 1, layer, 1)
            return run

        def q1_here(n, layer):
            return (layer == 0 and not (isinstance(n, int) and n == 0)) or (isinstance(n, int) and n == B)

        def added(g, i):
            return len(ADDED) * g + sum(a <= i for a in ADDED)

        def y_here(n):
            return not (isinstance(n, int) and n == 0)

        @block.sync
        def _(sp):
            for s in dma_signals:
                s.start(sp)

            def load_batch(b):
                sp.dma_start(ctx_sb[:, 0, :], ctxT[b, 0:P, :]).then_inc(ctx_in.sem, 16)
                sp.dma_start(ctx_sb[:, 1, :], ctxT[b, P:CD, :]).then_inc(ctx_in.sem, 16)
                sp.dma_start(x_sb[:, 0, :], xT[b, 0:P, :]).then_inc(x_in.sem, 16)
                sp.dma_start(x_sb[0:CT, 1, :], xT[b, P:C, :]).then_inc(x_in.sem, 16)

            def const(dst, src, arrived=weights_in):
                sp.dma_start(dst, src).then_inc(arrived, 16)

            const(wkt, wk_text.rearrange("(a p) c -> p a c", p=P), keys_in)
            const(wki, wk_ip.rearrange("(a p) c -> p a c", p=P), keys_in)
            load_batch(0)
            for layer in range(LAYERS):
                const(wq_sb[:, layer, 0, :], wq[layer, 0:P, :])
                const(wq_sb[0:CT, layer, 1, :], wq[layer, P:C, :])
            const(wvt, wv_text.rearrange("(a p) c -> p a c", p=P))
            const(wvi, wv_ip.rearrange("(a p) c -> p a c", p=P))
            const(id_f[:, :], ident)
            const(rows_sb[:, :], first_rows)
            const(pick_sb[:, :], den_pick)
            for layer in range(LAYERS):
                const(wo_sb[:, layer, :, :], wo[layer])
                const(bo_sb[:, layer, 0:1], bo[layer, 0:P].rearrange("(p a) -> p a", a=1))
                const(bo_sb[0:CT, layer, 1:2], bo[layer, P:C].rearrange("(p a) -> p a", a=1))
            const(mask_sb[:, 0, :], mask)

            def store_batch(b, load_next):
                for u, name in enumerate(UNITS):
                    if name == "s0":
                        if load_next:
                            sp.wait_ge(products.sem, products.at(b, pe_job["v4"]))
                            load_batch(b + 1)
                        sp.wait_ge(dve_prep.sem, dve_prep.at(b, dve_job["semq1"]))
                        sp.dma_start(sem_q_dram[b], sem_q_out).then_inc(sem_q_stored.sem, 16)
                    sp.wait_ge(split_done.sem, split_done.at(b, 2 * u + 2))
                    done = unit_stored[u].sem
                    src = parts[u]
                    if name in ("s0", "s1"):
                        h = int(name[1])
                        sp.dma_start(sem_k_dram[b, :, :, h * L:(h + 1) * L], src).then_inc(done, 16)
                        if name == "s1":
                            sp.dma_start(sem_k32_dram[b], sem_k32_out).then_inc(sem_k32_stored.sem, 16)
                        continue
                    for r in range(PARTS):
                        if name in ("k0", "k1"):
                            dst = k_stack[int(name[1]), b, r, :, 0:P, :]
                            sp.dma_start(dst.rearrange("i c k -> c i k"), src).then_inc(done, 16)
                        elif name == "krem":
                            for layer in range(LAYERS):
                                dst = k_stack[layer, b, r, :, P:C, :]
                                sp.dma_start(dst.rearrange("i c k -> c i k"),
                                             src[layer * CT:(layer + 1) * CT]).then_inc(done, 16)
                        else:
                            dst = q_stack[0, b, :, r, 0:P, :]
                            sp.dma_start(dst.rearrange("j c k -> c j k"), src[:, :, 0:S]).then_inc(done, 16)
                            dst = q_stack[0, b, :, r, P:C, :]
                            sp.dma_start(dst.rearrange("j c k -> c j k"), src[0:CT, :, S:2 * S]).then_inc(done, 16)

            def load_kq(layer, b, g):
                sp.dma_start(ks[0:STACK, g, :, :], k_stack[layer, b].rearrange(
                    "j i (d h) k -> (j i d) h k", d=D)[:, HG * g:HG * g + HG, :]).then_inc(kq_in[g].sem, 16)
                sp.dma_start(qs[0:STACK, g, :, :], q_stack[layer, b].rearrange(
                    "j i (d h) k -> (j i d) h k", d=D)[:, HG * g:HG * g + HG, :]).then_inc(kq_in[g].sem, 16)

            def load_sem_q(b, slot):
                sp.dma_start(sem_q[slot], sem_q_dram[b]).then_inc(sem_q_in.sem, 16)

            def load_sem_k(b, slot):
                sp.dma_start(sem_k[slot], sem_k_dram[b]).then_inc(sem_k_in.sem, 16)
                sp.dma_start(sem_k32[slot], sem_k32_dram[b]).then_inc(sem_k_in.sem, 16)

            def m_rows(n, g):
                sp.wait_ge(m_row_out.sem, m_row_out.at(n, g + 1))
                sp.dma_start(qs[MROW:KROWS, g, :, :], mrow[:, :].rearrange("r (a k) -> r a k", a=1)
                             .broadcast_to((MR, HG, S))).then_inc(m_row_in.sem, 16)

            sp.wait_ge(zeroed, 2)
            sp.dma_start(ks[MROW:KROWS, :, :, :].rearrange("r g j k -> r (g j k)"), key_kind).then_inc(kinds_in, 16)
            for g in range(NG):
                sp.dma_start(vtile[:, g, :, :, :], value_ones).then_inc(kinds_in, 16)
            store_batch(0, True)
            for s in (*unit_stored, sem_q_stored, sem_k32_stored):
                sp.wait_ge(s.sem, s.at(0, s.per))
            for g in range(NG - 1):
                load_kq(0, 0, g)
            load_sem_q(0, 0)
            load_sem_k(0, 0)
            with sp.Fori(1, B - 1) as b:
                store_batch(b, True)
            store_batch(B - 1, False)
            for s in (*unit_stored, sem_q_stored, sem_k32_stored):
                sp.wait_ge(s.sem, s.at(B - 1, s.per))
            load_kq(0, 0, NG - 1)
            m_rows(0, 0)

            def item(n, layer, slot):
                b = n - layer * B
                edge = isinstance(n, int)
                last_of_layer = edge and b == B - 1
                nxt = None if edge and n == ITEMS - 1 else ((1, 0) if last_of_layer else (layer, b + 1))
                for g in range(NG):
                    if g == 0 and layer == 0 and not last_of_layer:
                        sp.wait_ge(a_taken.sem, a_taken.at(n, 0))
                        if edge and n == 0:
                            sp.wait_ge(products.sem, products.at(B - 1, products.per))
                        load_sem_q(b + 1, 1 - slot)
                    if g >= 1 and nxt is not None:
                        sp.wait_ge(s_ready.sem, s_ready.at(n, HALVES * g))
                        if g == 1 and nxt[0] == 1:
                            sp.wait_ge(q1_stored.sem, q1_stored.at(nxt[1], 6))
                        load_kq(*nxt, g - 1)
                    elif g == 0 and not (edge and n == 0):
                        sp.wait_ge(s_ready.sem, s_ready.at(n, 0))
                        load_kq(layer, b, NG - 1)
                    if g == 1 and layer == 0 and not last_of_layer:
                        sp.wait_ge(s_added.sem, s_added.at(n, 1))
                        load_sem_k(b + 1, 1 - slot)
                    if g < NG - 1:
                        m_rows(n, g + 1)
                    elif nxt is not None:
                        m_rows(n + 1, 0)
                    if g == 3 and y_here(n):
                        store_y(n - 1, 0 if edge and n == B else layer)
                    if g == 3:
                        sp.wait_ge(y_ready.sem, y_ready.at(n, 0))
                        if layer == 1:
                            sp.wait_ge(y_stored.sem, y_stored.at(b, 2))
                        src = xT if layer == 0 else x1_dram
                        sp.dma_start(res[:, 0, :], src[b, 0:P, :]).then_inc(res_in.sem, 16)
                        sp.dma_start(res[0:CT, 1, :], src[b, P:C, :]).then_inc(res_in.sem, 16)
                    if g == 4 and q1_here(n, layer):
                        sp.wait_ge(q1_split.sem, q1_split.at(n - 1, 2))
                        for r in range(PARTS):
                            sp.dma_start(q_stack[1, n - 1, :, r, 0:P, :].rearrange("j c k -> c j k"),
                                         q_parts[:, :, 0:S]).then_inc(q1_stored.sem, 16)
                            sp.dma_start(q_stack[1, n - 1, :, r, P:C, :].rearrange("j c k -> c j k"),
                                         q_parts[0:CT, :, S:2 * S]).then_inc(q1_stored.sem, 16)

            def store_y(n, layer):
                sp.wait_ge(y_ready.sem, y_ready.at(n, 2))
                dst = (x1_dram if layer == 0 else out)[n - layer * B]
                sp.dma_start(dst[0:P, :], y_sb[:, 0, :]).then_inc(y_stored.sem, 16)
                sp.dma_start(dst[P:C, :], y_sb[0:CT, 1, :]).then_inc(y_stored.sem, 16)

            passes(item)(sp)
            store_y(ITEMS - 1, 1)
            sp.wait_ge(y_stored.sem, y_stored.at(ITEMS - 1, 2))

        @block.gpsimd
        def _(pool):
            for s in pool_signals:
                s.start(pool)
            pool.memset(mask_sb[:, 1, :], 1.0).then_inc(pool_init, 1)
            pool.memset(inv_wide[:, :, :, :], 0.0).then_inc(pool_init, 1)
            with pool.Fori(0, B) as b:
                for u, name in enumerate(UNITS):
                    pool.wait_ge(dve_prep.sem, dve_prep.at(b, dve_job[name + "_r"]))
                    pool.wait_ge(unit_stored[u].sem, unit_stored[u].at(b, 0))
                    pool.sem_inc(waited_pool, 1)
                    pool.tensor_copy(parts[u][:, 1, :], rest[u]).then_inc(split_done.sem, 1)
                    pool.wait_ge(split_done.sem, split_done.at(b, 2 * u + 1))
                    pool.tensor_tensor(parts[u][:, 2, :], rest[u], parts[u][:, 1, :],
                                       ALU.subtract).then_inc(split_done.sem, 1)

            def place_values(n, layer, b, g):
                cols = slice(HG * D * g, HG * D * (g + 1))

                def v(k0, k1):
                    return vals[:, layer, bass.ds(b, 1), k0:k1, cols].rearrange(
                        "p a k (h d) -> p (a k) h d", h=HG)
                pool.sem_inc(waited_pool, 1)
                pool.tensor_copy(vtile[:, g, 0:1, :, 0:D], v(0, 1))
                pool.tensor_copy(vtile[:, g, :, :, IPC:IPC + D], v(1, KC + 1)).then_inc(v_placed.sem, 1)

            def split_max(n, g):
                pool.wait_ge(a_taken.sem, a_taken.at(n, HG * (g + 1)))
                pool.wait_ge(m_turned.sem, m_turned.at(n, g))
                pool.sem_inc(waited_pool, 1)
                s = m_split.sem
                at = 4 * g

                def part(i):
                    return mpart[:, :, :, i, :]
                mxg = mx[:, g, :, :, :]
                r1 = mres[:, :, :, :]
                pool.tensor_copy(part(0), mxg).then_inc(s, 1)
                pool.wait_ge(m_split.sem, m_split.at(n, at + 1))
                pool.tensor_tensor(r1, mxg, part(0), ALU.subtract).then_inc(s, 1)
                pool.wait_ge(m_split.sem, m_split.at(n, at + 2))
                pool.sem_inc(waited_pool, 1)
                pool.tensor_copy(part(1), r1).then_inc(s, 1)
                pool.wait_ge(m_split.sem, m_split.at(n, at + 3))
                pool.tensor_tensor(part(2), r1, part(1), ALU.subtract).then_inc(s, 1)

            def widen(n, layer, g):
                pool.wait_ge(inv_ready.sem, inv_ready.at(n, g + 1))
                pool.wait_ge(scale_ready.sem, scale_ready.at(n, g))
                pool.sem_inc(waited_pool, 1)
                shape = (P, QT, HG, IPC)
                pool.tensor_copy(inv_wide[:, :, :, 0:IPC], inv[:, :, :, 0:1].broadcast_to(shape))
                pool.tensor_tensor(inv_wide[:, :, :, IPC:2 * IPC], inv[:, :, :, 1:2].broadcast_to(shape),
                                   mask_sb[:, layer, :].rearrange("p (t a b) -> p t a b", a=1, b=1)
                                   .broadcast_to(shape), ALU.mult).then_inc(inv_widened.sem, 1)

            pool.wait_ge(weights_in, N_WEIGHTS * 16)
            for s in (act_prep,):
                pool.wait_ge(s.sem, s.at(B - 1, act_job["s1_hi"]))
            pool.wait_ge(kinds_in, (1 + NG) * 16)
            for g in range(NG - 2):
                place_values(0, 0, 0, g)
            split_max(0, 0)

            def item(n, layer, slot):
                b = n - layer * B
                edge = isinstance(n, int)
                last_of_layer = edge and b == B - 1
                nxt = None if edge and n == ITEMS - 1 else ((1, 0) if last_of_layer else (layer, b + 1))
                for g in range(NG):
                    if g > 1:
                        widen(n, layer, g - 2)
                    elif not (edge and n == 0):
                        widen(n - 1, 0 if edge and n == B else layer, g + NG - 2)
                    if g < NG - 1:
                        split_max(n, g + 1)
                    elif nxt is not None:
                        split_max(n + 1, 0)
                    if g < 2:
                        if not (edge and n == 0):
                            pool.wait_ge(pv_ready.sem, pv_ready.at(n - 1, g + NG - 1))
                        place_values(n, layer, b, g + NG - 2)
                    elif nxt is not None:
                        pool.wait_ge(pv_ready.sem, pv_ready.at(n, g - 1))
                        place_values(n + 1, *nxt, g - 2)
                    if g == 4 and q1_here(n, layer):
                        pool.wait_ge(q1_rest.sem, q1_rest.at(n - 1, 1))
                        pool.wait_ge(q1_stored.sem, q1_stored.at(n - 1, 0))
                        pool.sem_inc(waited_pool, 1)
                        pool.tensor_copy(q_parts[:, 1, :], q_rest[:, :]).then_inc(q1_split.sem, 1)
                        pool.wait_ge(q1_split.sem, q1_split.at(n - 1, 1))
                        pool.tensor_tensor(q_parts[:, 2, :], q_rest[:, :], q_parts[:, 1, :],
                                           ALU.subtract).then_inc(q1_split.sem, 1)

            passes(item)(pool)
            widen(ITEMS - 1, 1, NG - 2)
            widen(ITEMS - 1, 1, NG - 1)

        @block.tensor
        def _(pe):
            for s in pe_signals:
                s.start(pe)
            pe.wait_ge(keys_in, 2 * 16)

            def free_bank(b, name):
                last = {"k0": ("a", "e1", 0), "krem": ("a", "v3", 0), "q": ("a", "v4", 0), "k1": ("a", "pT", 0),
                        "gram": ("d", "semq0", 0), "v0": ("d", "semq1", 0), "v1": ("d", "s0_r", 0),
                        "v2": ("d", "s1_r", 0), "txt": ("d", "k0_r", 1), "v3": ("d", "krem_r", 1),
                        "v4": ("d", "q_r", 1), "pT": ("d", "k1_r", 1), "semq0": ("a", "gram", 1),
                        "semq1": ("a", "v0", 1), "s0": ("a", "v1", 1), "s1": ("a", "v2", 1)}[name]
                sig, jobs = (act_prep, act_job) if last[0] == "a" else (dve_prep, dve_job)
                pe.wait_ge(sig.sem, sig.at(b, jobs[last[1]] - (0 if last[2] else sig.per)))

            def done(mm):
                mm.then_inc(products.sem, 1)

            pe.wait_ge(gram_zeroed, 1)
            with pe.Fori(0, B) as b:
                def keys(name, cols):
                    o = pbank[(pe_job[name] - 1) % 8]
                    free_bank(b, name)
                    for w, ks_ in ((wkt, slice(0, T)), (wki, slice(T, L))):
                        for a in range(2):
                            mm = pe.matmul(o[:, ks_], w[:, a, cols], ctx_sb[:, a, ks_],
                                           start=(a == 0), stop=(a == 1))
                    done(mm)

                def values(i):
                    name = f"v{i}"
                    o = pbank[(pe_job[name] - 1) % 8][:, 0:LAYERS * C]
                    free_bank(b, name)
                    w = wvt if i == 0 else wvi
                    c = max(i - 1, 0)
                    for a in range(2):
                        mm = pe.matmul(o, ctx_sb[:, a, c * P:(c + 1) * P], w[:, a, :],
                                       start=(a == 0), stop=(a == 1))
                    done(mm)

                pe.wait_ge(ctx_in.sem, ctx_in.at(b, 2))
                keys("k0", slice(0, P))
                keys("krem", slice(2 * P, 3 * P))
                free_bank(b, "q")
                pe.wait_ge(weights_in, N_WEIGHTS * 16)
                pe.wait_ge(x_in.sem, x_in.at(b, 2))
                o = pbank[2].rearrange("p (a s) -> p a s", a=2)
                for m in range(2):
                    pe.matmul(o[:, m, :], wq_sb[:, 0, 0, m * P:(m + 1) * P], x_sb[:, 0, :], start=True, stop=False)
                    mm = pe.matmul(o[:, m, :], wq_sb[0:CT, 0, 1, m * P:(m + 1) * P], x_sb[0:CT, 1, :],
                                   start=False, stop=True)
                done(mm)
                keys("k1", slice(P, 2 * P))
                free_bank(b, "gram")
                for a in range(2):
                    mm = pe.matmul(pbank[4][0:T, T:L], ctx_sb[:, a, 0:T], ctx_sb[:, a, T:L],
                                   start=(a == 0), stop=(a == 1))
                done(mm)
                for i in range(3):
                    values(i)
                free_bank(b, "txt")
                pe.wait_ge(act_prep.sem, act_prep.at(b, act_job["q_32"]))
                for t in range(QT):
                    pe.matmul(pbank[0][:, t * T:(t + 1) * T], qt32[:, 0, t * P:(t + 1) * P], kt32[:, 0, :],
                              start=True, stop=False)
                    mm = pe.matmul(pbank[0][:, t * T:(t + 1) * T], qt32[0:CT, 1, t * P:(t + 1) * P],
                                   kt32[0:CT, 1, :], start=False, stop=True)
                done(mm)
                values(3)
                values(4)
                free_bank(b, "pT")
                pe.wait_ge(dve_prep.sem, dve_prep.at(b, dve_job["p1"]))
                for t in range(QT):
                    mm = pe.transpose(pbank[3][0:T, t * P:(t + 1) * P], p_txt[:, t, :], id_f[:, :])
                done(mm)
                pe.wait_ge(act_prep.sem, act_prep.at(b, act_job["pT"]))
                for t in range(QT):
                    free_bank(b, f"semq{t}")
                    done(pe.matmul(pbank[4 + t][:, 0:L - T], pT_txt[:, t * P:(t + 1) * P], gram[:, T:L],
                                   start=True, stop=True))
                for h in range(2):
                    free_bank(b, f"s{h}")
                    for c in range(2):
                        k = 2 * h + c
                        mm = pe.matmul(pbank[6 + h][:, c * S:(c + 1) * S], gram[:, k * P:(k + 1) * P],
                                       pT_txt[:, :], start=True, stop=True)
                    done(mm)

            pe.wait_ge(act_prep.sem, act_prep.at(B - 1, act_job["pT"]))
            pe.wait_ge(dve_prep.sem, dve_prep.at(B - 1, dve_job["nmax"]))
            pe.wait_ge(id_b_ready, 1)
            pe.wait_ge(zeroed, 2)
            pe.wait_ge(kinds_in, (1 + NG) * 16)

            def by_query(n, g, i):
                if i == 0:
                    pe.wait_ge(kq_in[g].sem, kq_in[g].at(n, 2))
                j, t = divmod(i, QT)
                if t == 0:
                    pe.wait_ge(a_taken.sem, a_taken.at(n, HG * g + j - 1))
                mm = pe.matmul(by_query_bank[j % 2][:, t, :], qs[0:MROW, g, j, t * P:(t + 1) * P],
                               ks[0:MROW, g, j, :], start=True, stop=True)
                if t == QT - 1:
                    mm.then_inc(a_ready.sem, 1)

            def bank_read(n, layer, g, i):
                if layer == 0 and (i + 6) % 8 in ADDED:
                    pe.wait_ge(s_added.sem, s_added.at(n, added(g, i - 2) if i >= 2 else added(g - 1, i + 6)))
                else:
                    pe.wait_ge(probs_ready.sem, probs_ready.at(n, HALVES * g + i - 1))

            def by_key(n, layer, g, i, slot, turned=True):
                j, part = divmod(i, 2)
                o = by_key_bank[i % 2]
                here = layer == 0 and i not in ADDED
                if i == 0:
                    pe.wait_ge(m_row_in.sem, m_row_in.at(n, g + 1))
                if g == 0 and here and i == 1:
                    pe.wait_ge(sem_k_in.sem, sem_k_in.at(n, 2))
                if i == TURN + 1 and turned:
                    pe.wait_ge(m_row_out.sem, m_row_out.at(n, g + 2))
                else:
                    bank_read(n, layer, g, i)
                for c in range(2):
                    k = 2 * part + c
                    mm = pe.matmul(o[:, c * S:(c + 1) * S], ks[0:KROWS, g, j, k * P:(k + 1) * P],
                                   qs[0:KROWS, g, j, :], start=(not here or c == 0), stop=not here,
                                   skip_group_check=here)
                if here:
                    for p in range(PARTS):
                        mm = pe.matmul(o[:, :], id_b[:, :], sem_k[slot][:, p, part * L:(part + 1) * L],
                                       start=False, stop=(p == PARTS - 1), skip_group_check=True)
                mm.then_inc(s_ready.sem, 1)

            def times_values(n, g, *chunks):
                if 0 in chunks:
                    pe.wait_ge(probs_ready.sem, probs_ready.at(n, HALVES * (g + 1)))
                    pe.wait_ge(hs_ready.sem, hs_ready.at(n, g))
                    pe.wait_ge(v_placed.sem, v_placed.at(n, g + 1))
                for c in chunks:
                    for j in range(HG):
                        mm = pe.matmul(pv_bank[VW * j:VW * (j + 1), 0:S], vtile[:, g, c, j, :],
                                       probs[:, (HG * g + j) % RING, c * S:(c + 1) * S],
                                       start=(c == 0), stop=(c == KC - 1))
                if KC - 1 in chunks:
                    mm.then_inc(pv_ready.sem, 1)

            def denominators(n, g):
                pe.wait_ge(pv_copied.sem, pv_copied.at(n, g + 1))
                for t in range(QT):
                    mm = pe.matmul(den[:, t * 2 * HG:(t + 1) * 2 * HG], hs[:, g, t * P:(t + 1) * P],
                                   pick_sb[:, :], start=True, stop=True)
                mm.then_inc(den_ready.sem, 1)

            def turn_inverses(n, g):
                pe.wait_ge(inv_widened.sem, inv_widened.at(n, g + 1))
                for t in range(QT):
                    mm = pe.transpose(scale_rows[:, t * P:(t + 1) * P],
                                      inv_wide[:, t, :, :].rearrange("p h r -> p (h r)"), id_f[:, :])
                mm.then_inc(scale_ready.sem, 1)

            def turn_max(n, g):
                pe.wait_ge(m_split.sem, m_split.at(n, 4 * (g + 1)))
                pe.wait_ge(m_row_out.sem, m_row_out.at(n, g))
                for t in range(QT):
                    mm = pe.transpose(turned_max[:, t * P:(t + 1) * P],
                                      mpart[:, t, :, :, :].rearrange("p a b c -> p (a b c)"), id_b[:, :])
                mm.then_inc(m_turned.sem, 1)

            def project_out(n, layer, g):
                pe.wait_ge(hs_ready.sem, hs_ready.at(n, g + 1))
                for m, (c0, c1) in enumerate(((0, P), (P, C))):
                    mm = pe.matmul(misc[0:c1 - c0, m * S:(m + 1) * S], wo_sb[:, layer, g, c0:c1],
                                   hs[:, g, :], start=(g == 0 and m == 0), stop=(g == NG - 1),
                                   skip_group_check=True)
                if g == NG - 1:
                    mm.then_inc(y_mm.sem, 1)

            def project_q1(n):
                pe.wait_ge(y_ready.sem, y_ready.at(n, 2))
                for m in range(2):
                    o = misc[:, m * S:(m + 1) * S]
                    pe.matmul(o, wq_sb[:, 1, 0, m * P:(m + 1) * P], y_sb[:, 0, :], start=True, stop=False)
                    mm = pe.matmul(o, wq_sb[0:CT, 1, 1, m * P:(m + 1) * P], y_sb[0:CT, 1, :],
                                   start=False, stop=True)
                mm.then_inc(q1_mm.sem, 1)

            for i in range(QT * HG):
                by_query(0, 0, i)
            pe.wait_ge(dve_prep.sem, dve_prep.at(B - 1, dve_prep.per))
            for i in range(QT * HG):
                by_query(0, 1, i)
            turn_max(0, 0)

            def item(n, layer, slot):
                edge = isinstance(n, int)
                final = edge and n == ITEMS - 1
                layer_before = 0 if edge and n == B else layer
                for g in range(NG):
                    ahead = (n, g + 2) if g + 2 < NG else (None if final else (n + 1, g + 2 - NG))
                    before = (n, g - 1) if g > 0 else (None if edge and n == 0 else (n - 1, NG - 1))
                    before2 = (n, g - 2) if g > 1 else (None if edge and n == 0 else (n - 1, g + NG - 2))
                    for i in range(HALVES):
                        by_key(n, layer, g, i, slot, turned=not (final and g == NG - 1))
                        if i == TURN and not (final and g == NG - 1):
                            bank_read(n, layer, g, TURN + 1)
                            if g < NG - 1:
                                turn_max(n, g + 1)
                            else:
                                turn_max(n + 1, 0)
                        if i == 6 and before:
                            denominators(*before)
                        if ahead:
                            by_query(*ahead, i)
                        if i == 2 and before2:
                            turn_inverses(*before2)
                        if i in (3, 4) and before:
                            times_values(*before, *((0, 1) if i == 3 else (2, 3)))
                        if i == 5 and g == 2 and q1_here(n, layer):
                            project_q1(n - 1)
                        if i == 7 and g < 2 and y_here(n):
                            project_out(n - 1, layer_before, g + NG - 2)
                        if i == 5 and g == 3:
                            if y_here(n):
                                pe.wait_ge(y_ready.sem, y_ready.at(n - 1, 2))
                            if q1_here(n, layer):
                                pe.wait_ge(q1_rest.sem, q1_rest.at(n - 1, 1))
                            project_out(n, layer, 0)
                        if i == 7 and g >= 3:
                            project_out(n, layer, g - 2)

            passes(item)(pe)
            n = ITEMS - 1
            turn_inverses(n, NG - 2)
            times_values(n, NG - 1, *range(KC))
            project_out(n, 1, NG - 2)
            denominators(n, NG - 1)
            turn_inverses(n, NG - 1)
            project_out(n, 1, NG - 1)

        @block.scalar
        def _(act):
            for s in act_signals:
                s.start(act)
            act.wait_ge(weights_in, N_WEIGHTS * 16)
            act.activation(id_b[:, :], id_f[:, :], ACT.Copy).then_inc(id_b_ready, 1)

            with act.Fori(0, B) as b:
                def bank_of(name):
                    return pbank[(pe_job[name] - 1) % 8]

                def copy(name, dst, src, **kw):
                    return act.activation(dst, src, kw.pop("func", ACT.Copy), **kw).then_inc(act_prep.sem, 1)

                def high_part(u):
                    act.wait_ge(unit_stored[u].sem, unit_stored[u].at(b, 0))
                    copy("hi", parts[u][:, 0, :], bank_of(UNITS[u]))

                def values(i):
                    act.wait_ge(products.sem, products.at(b, pe_job[f"v{i}"]))
                    keep = {"scale": rows_sb[:, i:i + 1]} if i < 2 else {}
                    copy("v", vals[:, :, bass.ds(b, 1), i, :].rearrange("p l a c -> p (l a) c"),
                         bank_of(f"v{i}")[:, 0:LAYERS * C].rearrange("p (l c) -> p l c", l=LAYERS), **keep)

                act.wait_ge(products.sem, products.at(b, pe_job["k0"]))
                copy("k32", kt32[:, 0, :], bank_of("k0")[:, 0:T])
                high_part(0)
                act.wait_ge(products.sem, products.at(b, pe_job["krem"]))
                copy("k32", kt32[0:CT, 1, :], bank_of("krem")[0:CT, 0:T])
                high_part(1)
                act.wait_ge(products.sem, products.at(b, pe_job["q"]))
                copy("q32", qt32[:, :, :].rearrange("p a s -> p (a s)"), bank_of("q"))
                high_part(2)
                act.wait_ge(products.sem, products.at(b, pe_job["k1"]))
                high_part(3)
                act.wait_ge(products.sem, products.at(b, pe_job["gram"]))
                copy("gram", gram[:, T:L], bank_of("gram")[0:T, T:L], scale=SEM_SCALE)
                for i in range(3):
                    values(i)
                act.wait_ge(dve_prep.sem, dve_prep.at(b, dve_job["nmax"]))
                for t in range(QT):
                    copy("e", e_txt[:, t, :], bank_of("txt")[:, t * T:(t + 1) * T], func=ACT.Exp,
                         bias=stat[:, 1, t:t + 1], scale=SCALE, accum_out=stat[:, 2, t:t + 1])
                for i in range(3, 5):
                    values(i)
                act.wait_ge(products.sem, products.at(b, pe_job["pT"]))
                copy("pT", pT_txt[:, :], bank_of("pT")[0:T, 0:S])
                for h in range(2):
                    act.wait_ge(products.sem, products.at(b, pe_job[f"s{h}"]))
                    act.wait_ge(sem_k32_stored.sem, sem_k32_stored.at(b, 0))
                    copy("s32", sem_k32_out[:, h * L:(h + 1) * L], bank_of(f"s{h}"))
                    high_part(4 + h)

            for s in (*unit_stored, sem_k32_stored):
                act.wait_ge(s.sem, s.at(B - 1, s.per))
            act.wait_ge(split_done.sem, split_done.at(B - 1, split_done.per))

            def exponentials(n, layer, g, i):
                j, part = divmod(i, 2)
                place = probs[:, (HG * g + j) % RING, part * 512:(part + 1) * 512]
                if layer == 0 and i in ADDED:
                    act.wait_ge(s_added.sem, s_added.at(n, added(g, i)))
                    src = place
                else:
                    act.wait_ge(s_ready.sem, s_ready.at(n, HALVES * g + i + 1))
                    act.wait_ge(pv_ready.sem, pv_ready.at(n, (HG * g + j - RING) // HG + 1))
                    src = by_key_bank[i % 2][:, :]
                act.activation(place, src, ACT.Exp, scale=SCALE).then_inc(probs_ready.sem, 1)

            def take_m_rows(n, g):
                act.wait_ge(m_turned.sem, m_turned.at(n, g + 1))
                act.wait_ge(m_row_in.sem, m_row_in.at(n, g))
                act.activation(mrow[:, :], turned_max, ACT.Copy).then_inc(m_row_out.sem, 1)

            def copy_pv(n, g):
                act.wait_ge(pv_ready.sem, pv_ready.at(n, g + 1))
                act.activation(hs[:, g, :], pv_bank[:, 0:S], ACT.Copy).then_inc(pv_copied.sem, 1)

            take_m_rows(0, 0)

            def item(n, layer, slot):
                edge = isinstance(n, int)
                for g in range(NG):
                    for i in range(HALVES):
                        exponentials(n, layer, g, i)
                        if i == TURN - 1 and g < NG - 1:
                            take_m_rows(n, g + 1)
                        elif i == TURN - 1 and not (edge and n == ITEMS - 1):
                            take_m_rows(n + 1, 0)
                        if i == 5 and g > 0:
                            copy_pv(n, g - 1)
                        elif i == 5 and not (edge and n == 0):
                            copy_pv(n - 1, NG - 1)
                        if i == 6 and g == 2 and q1_here(n, layer):
                            act.wait_ge(q1_mm.sem, q1_mm.at(n - 1, 1))
                            act.wait_ge(q1_stored.sem, q1_stored.at(n - 1, 0))
                            act.activation(q_parts[:, 0, :], misc[:, :], ACT.Copy).then_inc(q1_hi.sem, 1)

            passes(item)(act)
            copy_pv(ITEMS - 1, NG - 1)

        @block.vector
        def _(dve):
            for s in dve_signals:
                s.start(dve)
            dve.memset(gram[:, 0:T], 0.0).then_inc(gram_zeroed, 1)
            for t in (ks, qs):
                dve.memset(t[:, :, :, :].rearrange("p g j k -> p (g j k)").bitcast(F32), 0.0).then_inc(zeroed, 1)
            dve.wait_ge(weights_in, N_WEIGHTS * 16)
            with dve.Fori(0, B) as b:
                def bank_of(name):
                    return pbank[(pe_job[name] - 1) % 8]

                def take_rest(u):
                    name = UNITS[u]
                    dve.wait_ge(act_prep.sem, act_prep.at(b, act_job[name + "_hi"]))
                    dve.wait_ge(split_done.sem, split_done.at(b, 2 * u + 2 - split_done.per))
                    dve.tensor_tensor(rest[u], bank_of(name), parts[u][:, 0, :], ALU.subtract)\
                        .then_inc(dve_prep.sem, 1)

                for u in range(4):
                    take_rest(u)
                dve.wait_ge(products.sem, products.at(b, pe_job["txt"]))
                dve.tensor_reduce(stat[:, 0, :], bank_of("txt")[:, 0:QT * T].rearrange("p (t k) -> p t k", t=QT),
                                  AX, ALU.max).then_inc(dve_prep.sem, 1)
                dve.wait_ge(dve_prep.sem, dve_prep.at(b, dve_job["max"]))
                dve.tensor_scalar(stat[:, 1, :], stat[:, 0, :], -SCALE, None, ALU.mult).then_inc(dve_prep.sem, 1)
                dve.wait_ge(act_prep.sem, act_prep.at(b, act_job["e1"]))
                dve.reciprocal(stat[:, 3, :], stat[:, 2, :]).then_inc(dve_prep.sem, 1)
                dve.wait_ge(dve_prep.sem, dve_prep.at(b, dve_job["rsum"]))
                for t in range(QT):
                    dve.tensor_scalar(p_txt[:, t, :], e_txt[:, t, :], stat[:, 3, t:t + 1], None, ALU.mult)\
                        .then_inc(dve_prep.sem, 1)
                dve.wait_ge(sem_q_stored.sem, sem_q_stored.at(b, 0))
                for t in range(QT):
                    dve.wait_ge(products.sem, products.at(b, pe_job[f"semq{t}"]))
                    dve.tensor_copy(sem_q_out[:, t, :], bank_of(f"semq{t}")[:, 0:L - T]).then_inc(dve_prep.sem, 1)
                for u in range(4, 6):
                    take_rest(u)

            def maxima(n, layer, g, j, slot):
                scores = by_query_bank[j % 2]
                if layer == 0 and g == 0 and j == 0:
                    dve.wait_ge(sem_q_in.sem, sem_q_in.at(n, 1))
                dve.wait_ge(a_ready.sem, a_ready.at(n, HG * g + j + 1))
                dve.tensor_reduce(mx[:, g, :, 0, j], scores[:, :, 0:T], AX, ALU.max)
                if layer == 0:
                    dve.wait_ge(a_taken.sem, a_taken.at(n, HG * g + j - 1))
                    for t in range(QT):
                        f0 = (QT * j + t) % FUSED * (L - T)
                        dve.sem_inc(waited_dve, 1)
                        last = dve.tensor_tensor_reduce(fused[:, f0:f0 + L - T], scores[:, t, T:L], sem_q[slot][:, t, :],
                                                        1.0, -3.0e38, ALU.add, ALU.max, mx[:, g, t, 1, j:j + 1])
                else:
                    last = dve.tensor_reduce(mx[:, g, :, 1, j], scores[:, :, T:L], AX, ALU.max)
                last.then_inc(a_taken.sem, 1)

            def invert(n, g):
                dve.wait_ge(den_ready.sem, den_ready.at(n, g + 1))
                dve.wait_ge(inv_widened.sem, inv_widened.at(n, g))
                dve.reciprocal(inv[:, :, :, :].rearrange("p t h k -> p (t h k)"), den).then_inc(inv_ready.sem, 1)

            def normalise(n, g):
                dve.wait_ge(scale_ready.sem, scale_ready.at(n, g + 1))
                dve.tensor_tensor(hs[:, g, :], hs[:, g, :], scale_rows, ALU.mult).then_inc(hs_ready.sem, 1)

            def add_semantic(n, g, i, slot):
                j, part = divmod(i, 2)
                if g == 0 and i == 0 and isinstance(n, int) and n == 0:
                    for s in (*unit_stored, sem_k32_stored):
                        dve.wait_ge(s.sem, s.at(B - 1, s.per))
                if g == 0 and i == 0:
                    dve.wait_ge(sem_k_in.sem, sem_k_in.at(n, 2))
                dve.wait_ge(s_ready.sem, s_ready.at(n, HALVES * g + i + 1))
                dve.wait_ge(pv_ready.sem, pv_ready.at(n, (HG * g + j - RING) // HG + 1))
                keys = slice(part * 512, (part + 1) * 512)
                dve.tensor_tensor(probs[:, (HG * g + j) % RING, keys], by_key_bank[i % 2][:, :],
                                  sem_k32[slot][:, keys], ALU.add).then_inc(s_added.sem, 1)

            def finish(n, layer):
                dve.wait_ge(y_mm.sem, y_mm.at(n, 1))
                dve.wait_ge(res_in.sem, res_in.at(n, 2))
                dve.wait_ge(y_stored.sem, y_stored.at(n, 0))
                for m, rows in enumerate((P, CT)):
                    dve.scalar_tensor_tensor(out=y_sb[0:rows, m, :], in0=misc[0:rows, m * S:(m + 1) * S],
                                             scalar=bo_sb[0:rows, layer, m:m + 1], in1=res[0:rows, m, :],
                                             op0=ALU.add, op1=ALU.add).then_inc(y_ready.sem, 1)

            dve.wait_ge(sem_q_stored.sem, sem_q_stored.at(B - 1, 1))
            for g in range(2):
                for j in range(HG):
                    maxima(0, 0, g, j, 0)

            def item(n, layer, slot):
                edge = isinstance(n, int)
                final = edge and n == ITEMS - 1
                next_layer = 1 if edge and n == B - 1 else layer
                for g in range(NG):
                    ahead = (n, layer, g + 2) if g + 2 < NG else (None if final else (n + 1, next_layer, g + 2 - NG))
                    before = (n, g - 1) if g > 0 else (None if edge and n == 0 else (n - 1, NG - 1))
                    before2 = (n, g - 2) if g > 1 else (None if edge and n == 0 else (n - 1, g + NG - 2))
                    for i in range(HALVES):
                        if layer == 0 and i in ADDED:
                            add_semantic(n, g, i, slot)
                        if i % 2 and ahead:
                            maxima(*ahead, i // 2, slot if g + 2 < NG else 1 - slot)
                        if i == 1 and before2:
                            normalise(*before2)
                        if i == 1 and g == 2 and y_here(n):
                            finish(n - 1, 0 if edge and n == B else layer)
                        if i == 6 and before:
                            invert(*before)
                    if g == 2 and q1_here(n, layer):
                        dve.wait_ge(q1_hi.sem, q1_hi.at(n - 1, 1))
                        dve.wait_ge(q1_split.sem, q1_split.at(n - 1, 0))
                        dve.tensor_tensor(q_rest[:, :], misc[:, :], q_parts[:, 0, :], ALU.subtract)\
                            .then_inc(q1_rest.sem, 1)

            passes(item)(dve)
            normalise(ITEMS - 1, NG - 2)
            invert(ITEMS - 1, NG - 1)
            normalise(ITEMS - 1, NG - 1)
            finish(ITEMS - 1, 1)


def kernel(x, ctx_2048, fside_S_0, L0_xattn_Wq, L0_xattn_Wk, L0_xattn_Wv, L0_xattn_Wk_ip, L0_xattn_Wv_ip,
           L0_xattn_Wout, L0_xattn_bout, L1_xattn_Wq, L1_xattn_Wk, L1_xattn_Wv, L1_xattn_Wk_ip,
           L1_xattn_Wv_ip, L1_xattn_Wo, L1_xattn_bo):
    import numpy as np
    import concourse.bacc as bacc
    from concourse.bass_utils import run_bass_kernel_spmd

    f = np.float32

    def dims_first(w):
        return np.asarray(w).reshape(w.shape[0], H, D).transpose(0, 2, 1).reshape(w.shape[0], C)

    def side_by_side(w0, w1):
        w0, w1 = dims_first(w0), dims_first(w1)
        pad = np.zeros((CD, 3 * P - 2 * C), f)
        return np.concatenate([w0[:, :P], w1[:, :P], w0[:, P:], w1[:, P:], pad], axis=1)

    def by_value_rows(w):
        rows = np.zeros((NG, HG, VW, C), f)
        w = np.asarray(w).reshape(NG, HG, D, C)
        rows[:, :, 0:D] = w
        rows[:, :, IPC:IPC + D] = w
        return rows.reshape(NG, P, C).transpose(1, 0, 2)

    wq = np.zeros((LAYERS, C, 2 * P), f)
    wq[0, :, :C] = dims_first(L0_xattn_Wq)
    wq[1, :, :C] = dims_first(np.asarray(L1_xattn_Wq).T)
    kind = np.zeros((2, PARTS, HG, NG, HG, L), f)
    for h in range(HG):
        kind[0, :, h, :, h, :T] = -1
        kind[1, :, h, :, h, T:] = -1
    ones = np.zeros((P, KC, VW), f)
    ones[:T, 0, D] = 1
    ones[T:, 0, IPC + D] = 1
    ones[:, 1:, IPC + D] = 1
    den_pick = np.zeros((P, HG, 2), f)
    for h in range(HG):
        den_pick[VW * h + D, h, 0] = 1
        den_pick[VW * h + IPC + D, h, 1] = 1
    first_rows = np.zeros((P, 2), f)
    first_rows[:T, 0] = 1
    first_rows[T:, 1] = 1
    arrays = {
        "xT": np.asarray(x).transpose(0, 2, 1),
        "ctxT": np.asarray(ctx_2048).transpose(0, 2, 1),
        "mask": np.asarray(fside_S_0).reshape(QT, P).T,
        "wk_text": side_by_side(L0_xattn_Wk, np.asarray(L1_xattn_Wk).T),
        "wk_ip": side_by_side(L0_xattn_Wk_ip, np.asarray(L1_xattn_Wk_ip).T),
        "wv_text": np.concatenate([np.asarray(L0_xattn_Wv), np.asarray(L1_xattn_Wv).T], axis=1),
        "wv_ip": np.concatenate([np.asarray(L0_xattn_Wv_ip), np.asarray(L1_xattn_Wv_ip).T], axis=1),
        "wq": wq,
        "wo": np.stack([by_value_rows(L0_xattn_Wout), by_value_rows(np.asarray(L1_xattn_Wo).T)]),
        "bo": np.stack([np.asarray(L0_xattn_bout), np.asarray(L1_xattn_bo)]),
        "ident": np.eye(P, dtype=f),
        "key_kind": kind.reshape(MR, H * L).astype(mybir.dt.np(BF16)),
        "value_ones": np.repeat(ones[:, :, None], HG, axis=2),
        "den_pick": den_pick.reshape(P, 2 * HG),
        "first_rows": first_rows,
    }
    arrays = {k: np.ascontiguousarray(v) for k, v in arrays.items()}
    nc = bacc.Bacc("TRN2", target_bir_lowering=False, num_devices=1)
    args = [nc.dram_tensor(k, v.shape, mybir.dt.from_np(v.dtype), kind="ExternalInput").ap()
            for k, v in arrays.items()]
    out = nc.dram_tensor("out", (B, C, S), F32, kind="ExternalOutput").ap()
    build(nc, *args, out)
    r = run_bass_kernel_spmd(nc, [arrays], core_ids=[0])
    return np.ascontiguousarray(r.results[0]["out"].transpose(0, 2, 1))
```

```python
from contextlib import ExitStack

import concourse.bass as bass
from concourse import mybir

F32 = mybir.dt.float32
BF16 = mybir.dt.bfloat16
ACT = mybir.ActivationFunctionType
ALU = mybir.AluOpType
AX = mybir.AxisListType.X

B, S, C, CD, L, T = 8, 256, 160, 256, 512, 77
H = 20
D = C // H
SCALE = float(D) ** -0.5
SEM_SCALE = 0.5
P = 128
LAYERS = 2
ITEMS = LAYERS * B
HG = 4
NG = H // HG
QT = S // P
KC = L // P
PARTS = 3
STACK = PARTS * PARTS * D
MROW = 96
MR = 2 * PARTS * HG
KROWS = MROW + MR
RING = 10
FUSED = 4
HALVES = 2 * HG
ADDED = (2, 6, 7)
POOLED = (0, 4)
STEPS = 2 * HALVES
TURN = (10, 6)
BESIDE = ((0, 3, 3, 4, 8, 9, 12, 14), (0, 0, 5, 6, 9, 9, 13, 13))
PE_TURN_O, PE_TURN_VALUES, PE_Q1 = ((4, 7), (15, 12), 15)
PE_PV = ((3, 7, 10, 11), (3, 4, 7, 9))
PE_OUT = (15, 14)
EXP_AT = ((8, 2, 4, 6, 14, 10, 12, 14), (0, 2, 4, 6, 8, 10, 12, 14))
ACT_TAKE, ACT_COPY, ACT_HI = ((9, 4), (10, 8), 15)
DVE_WEIGH, DVE_FINISH, DVE_REST = ((15, 10), 1, 15)
DVE_MAX = ((2, 4, 7, 8, 9, 9, 14, 15), (3, 7, 10, 14))
POOL_JOIN, POOL_SPLIT, POOL_PLACE, POOL_Q1 = ((0, 0), (0, 0), (0, 3), (0, 0))
PE_YT, ACT_YT, POOL_BIAS, ACT_OT = (5, 6, 3, 6)
VW = 32
IPC = 9


class Signal:

    def __init__(self, sem, per, unit=1):
        self.sem, self.per, self.unit = sem, per, unit

    def start(self, eng):
        eng.sem_inc(self.sem, self.per * self.unit)

    def at(self, turn, count):
        return turn * (self.per * self.unit) + (self.per + count) * self.unit


def build(nc, x, xT, ctxT, mask, wk_text, wk_ip, wv_text, wv_ip, wq, wo, bo,
          ident, key_kind, value_ones, first_rows, out):
    k_stack = nc.dram_tensor("k_stack", (LAYERS, B, PARTS, PARTS, D * H, L), BF16, kind="Internal").ap()
    q_stack = nc.dram_tensor("q_stack", (LAYERS, B, PARTS, PARTS, D * H, S), BF16, kind="Internal").ap()
    sem_q_dram = nc.dram_tensor("sem_q_dram", (B, P, QT, L - T), F32, kind="Internal").ap()
    sem_k_dram = nc.dram_tensor("sem_k_dram", (B, P, PARTS, KC * S), BF16, kind="Internal").ap()
    sem_k32_dram = nc.dram_tensor("sem_k32_dram", (B, P, KC * S), F32, kind="Internal").ap()
    x1_dram = nc.dram_tensor("x1_dram", (B, S, C), F32, kind="Internal").ap()
    CT = C - P

    with ExitStack() as ctx:
        def sb(name, shape, dt=F32):
            return ctx.enter_context(nc.sbuf_tensor(name, shape, dt))

        def sem(name):
            return ctx.enter_context(nc.semaphore(name))

        wk_sb = sb("wk_sb", [P, 2, 2, 3 * P])
        wv_sb = sb("wv_sb", [P, 2, 2, LAYERS * C])
        wkt, wki, wvt, wvi = wk_sb[:, 0], wk_sb[:, 1], wv_sb[:, 0], wv_sb[:, 1]
        wq_sb = sb("wq_sb", [P, LAYERS, 2, 2 * P])
        wo_sb = sb("wo_sb", [P, LAYERS, 2, C])
        bo_sb = sb("bo_sb", [P, LAYERS, C])
        id_f = sb("id_f", [P, P])
        id_b = sb("id_b", [P, P], BF16)
        rows_sb = sb("rows_sb", [P, 2])
        mask_sb = sb("mask_sb", [P, LAYERS, QT])
        ctx_sb = sb("ctx_sb", [P, 2, L])
        x_sb = sb("x_sb", [P, 2, S])
        kt32 = sb("kt32", [P, 2, T])
        qt32 = sb("qt32", [P, 2, S])
        gram = sb("gram", [T, L])
        e_txt = sb("e_txt", [P, QT, T])
        p_txt = sb("p_txt", [P, QT, T])
        pT_txt = sb("pT_txt", [T, S])
        stat = sb("stat", [P, 4, QT])
        ks = sb("ks", [P, NG, HG, L], BF16)
        qs = sb("qs", [P, NG, HG, S], BF16)
        vals = sb("vals", [P, LAYERS, B, KC + 1, C])
        vtile = sb("vtile", [P, NG, KC, HG, VW])
        probs = sb("probs", [P, RING, KC * S])
        sem_q_first = sb("sem_q", [P, QT, L - T])
        sem_k_first = sb("sem_k", [P, PARTS, KC * S], BF16)
        fused = sb("fused", [P, FUSED * (L - T)], BF16)
        mx = sb("mx", [P, NG, QT, 2, HG])
        mres = sb("mres", [P, QT, 2, HG])
        mpart = sb("mpart", [P, QT, 2, PARTS, HG], BF16)
        mrow = sb("mrow", [MR, S], BF16)
        inv = sb("inv", [P, QT * HG, 2, 1])
        weighed = sb("weighed", [P, QT * HG, 2, D])
        o_sb = sb("o_sb", [P, QT, NG, HG, D])
        oT = sb("oT", [P, 2, S])
        sem_k32_first = sb("sem_k32", [P, KC * S])
        sums = sb("sums", [P, NG, S])
        res = sb("res", [P, QT, C])
        y_sb = sb("y_sb", [P, QT, C])
        q_parts = sb("q_parts", [P, PARTS, 2 * S], BF16)
        q_rest = sb("q_rest", [P, 2 * S])

        UNITS = ["k0", "krem", "q", "k1", "s0", "s1"]
        flat = probs[:, :, :].rearrange("p a b -> p (a b)")
        half = PARTS * L // 2
        parts = [flat[:, u * half:(u + 1) * half].bitcast(BF16).rearrange("p (a b) -> p a b", a=PARTS)
                 for u in range(6)]
        rest = [flat[:, 6 * half + u * L:6 * half + (u + 1) * L] for u in range(6)]

        ctx_slot = [ctx_sb[:, :, :], sums[:, 0:2 * L // S, :].rearrange("p a b -> p (a b)").rearrange(
            "p (a l) -> p a l", a=2)]
        x_slot = [x_sb[:, :, :], q_rest[:, :].rearrange("p (a s) -> p a s", a=2)]
        yT = x_sb

        sem_k32_out = flat[:, 6 * (half + L):6 * (half + L) + KC * S]
        sem_q_out = fused[:, :].bitcast(F32).rearrange("p (t k) -> p t k", t=QT)

        sem_q = [sem_q_first[:, :, :], ctx_sb[:, :, :].rearrange("p a b -> p (a b)")[:, 0:QT * (L - T)]
                 .rearrange("p (t k) -> p t k", t=QT)]
        sem_k = [sem_k_first[:, :, :], wk_sb[:, :, :, :].rearrange("p a b c -> p (a b c)").bitcast(BF16)
                 .rearrange("p (a b) -> p a b", a=PARTS)]
        sem_k32 = [sem_k32_first[:, :], wv_sb[:, :, :, :].rearrange("p a b c -> p (a b c)")[:, 0:KC * S]]

        by_query_bank = [ctx.enter_context(nc.psum_tensor(f"by_query{i}", [P, QT, 512], F32)) for i in range(2)]
        by_key_bank = [ctx.enter_context(nc.psum_tensor(f"by_key{i}", [P, 512], F32)) for i in range(2)]
        pv_bank = ctx.enter_context(nc.psum_tensor("pv_bank", [P, 512], F32))
        misc = ctx.enter_context(nc.psum_tensor("misc", [P, 512], F32))
        pbank = [by_query_bank[0][:, 0, :], by_query_bank[0][:, 1, :], by_query_bank[1][:, 0, :],
                 by_query_bank[1][:, 1, :], by_key_bank[0][:, :], by_key_bank[1][:, :], pv_bank[:, :], misc[:, :]]
        turned_max = by_key_bank[0][0:MR, 0:S // 2].bitcast(BF16)
        turned = pv_bank[:, S:2 * S].rearrange("p (a r) -> p a r", r=VW)
        values_turned = turned[:, :, 0:2 * IPC].rearrange("p a (k r) -> p a k r", k=2)[:, :, :, 0:D]
        den_turned = turned[:, :, 0:2 * IPC].rearrange("p a (k r) -> p a k r", k=2)[:, :, :, D:IPC]

        keys_in = sem("keys_in")
        weights_in = sem("weights_in")
        zeroed = sem("zeroed")
        gram_zeroed = sem("gram_zeroed")
        pool_init = sem("pool_init")
        kinds_in = sem("kinds_in")
        id_b_ready = sem("id_b_ready")
        waited_pool = sem("waited_pool")
        waited_dve = sem("waited_dve")
        ctx_in = [Signal(sem(f"ctx_in{i}"), 2, 16) for i in range(2)]
        x_in = [Signal(sem(f"x_in{i}"), 2, 16) for i in range(2)]
        products = Signal(sem("products"), 16)
        act_prep = Signal(sem("act_prep"), 20)
        dve_prep = Signal(sem("dve_prep"), 19)
        split_done = Signal(sem("split_done"), 6)
        unit_stored = [Signal(sem(f"stored_{u}"), k, 16) for u, k in zip(UNITS, (3, 6, 6, 3, 1, 1))]
        sem_q_stored = Signal(sem("sem_q_stored"), 1, 16)
        sem_k32_stored = Signal(sem("sem_k32_stored"), 1, 16)
        prep_signals = [*ctx_in, *x_in, products, act_prep, dve_prep, split_done, sem_q_stored, sem_k32_stored, *unit_stored]
        kq_in = [Signal(sem(f"kq_in{g}"), 2, 16) for g in range(NG)]
        a_ready = Signal(sem("a_ready"), H)
        a_taken = Signal(sem("a_taken"), H)
        m_split = Signal(sem("m_split"), 4 * NG)
        m_turned = Signal(sem("m_turned"), NG)
        m_row_out = Signal(sem("m_row_out"), NG)
        m_row_in = Signal(sem("m_row_in"), NG, 16)
        s_ready = Signal(sem("s_ready"), HALVES * NG)
        probs_ready = Signal(sem("probs_ready"), HALVES * NG)
        v_placed = Signal(sem("v_placed"), NG)
        pv_ready = Signal(sem("pv_ready"), NG)
        pv_copied = Signal(sem("pv_copied"), NG)
        values_ready = Signal(sem("values_ready"), NG)
        inv_ready = Signal(sem("inv_ready"), NG)
        joined = Signal(sem("joined"), 2 * NG)
        o_turned = Signal(sem("o_turned"), 1)
        oT_ready = Signal(sem("oT_ready"), 2)
        s_added = Signal(sem("s_added"), len(ADDED) * NG)
        s_pooled = Signal(sem("s_pooled"), len(POOLED) * NG)
        s_copied = Signal(sem("s_copied"), len(POOLED) * NG)
        weighed_ready = Signal(sem("weighed_ready"), NG)
        sem_q_in = Signal(sem("sem_q_in"), 1, 16)
        sem_k_in = Signal(sem("sem_k_in"), 2, 16)
        res_in = Signal(sem("res_in"), 1, 16)
        res_biased = Signal(sem("res_biased"), 1)
        y_turned = Signal(sem("y_turned"), 1)
        yT_ready = Signal(sem("yT_ready"), 2)
        y_mm = Signal(sem("y_mm"), 1)
        y_ready = Signal(sem("y_ready"), 1)
        y_stored = Signal(sem("y_stored"), 1, 16)
        q1_mm = Signal(sem("q1_mm"), 1)
        q1_hi = Signal(sem("q1_hi"), 1)
        q1_rest = Signal(sem("q1_rest"), 1)
        q1_split = Signal(sem("q1_split"), 2)
        q1_stored = Signal(sem("q1_stored"), 6, 16)
        pe_signals = [a_ready, m_turned, s_ready, pv_ready, values_ready, o_turned, y_turned, y_mm, q1_mm, products]
        act_signals = [*([s_copied] if POOLED else []), act_prep, m_row_out, probs_ready, pv_copied, oT_ready, yT_ready, q1_hi]
        dve_signals = [dve_prep, a_taken, s_added, inv_ready, weighed_ready, y_ready, q1_rest]
        pool_signals = [*([s_pooled] if POOLED else []), split_done, m_split, v_placed, joined, res_biased, q1_split]
        dma_signals = [*ctx_in, *x_in, *unit_stored, sem_q_stored, sem_k32_stored, *kq_in, m_row_in, sem_q_in, sem_k_in,
                       res_in, y_stored, q1_stored]

        N_WEIGHTS = 6 + 4 * LAYERS
        pe_job = {n: i + 1 for i, n in enumerate(
            ["k0", "krem", "q", "gram", "txt", "v0", "v1", "v2",
             "v3", "v4", "pT", "k1", "semq0", "semq1", "s0", "s1"])}
        act_job = {n: i + 1 for i, n in enumerate(
            ["k0_32", "k0_hi", "krem_32", "krem_hi", "q_32", "q_hi", "gram", "v0", "e0", "e1",
             "v1", "v2", "v3", "v4", "pT", "k1_hi", "s0_32", "s0_hi", "s1_32", "s1_hi"])}
        dve_job = {n: i + 1 for i, n in enumerate(
            ["k0_r", "k0_mid", "krem_r", "krem_mid", "q_r", "q_mid", "max", "nmax", "rsum",
             "p0", "p1", "k1_r", "k1_mid", "semq0", "semq1", "s0_r", "s0_mid", "s1_r", "s1_mid"])}
        last_reader = {"gram": "gram", "txt": "e1", "pT": "pT", **{f"v{i}": f"v{i}" for i in range(5)},
                       "semq0": "semq0", "semq1": "semq1", **{u: u + "_r" for u in UNITS}}

        block = ctx.enter_context(nc.Block())

        def passes(item):
            def run(eng):
                for layer in range(LAYERS):
                    n0 = layer * B
                    item(n0, layer, 0)
                    if layer == 0:
                        with eng.Fori(0, (B - 2) // 2) as pair:
                            item(pair * 2 + 1, layer, 1)
                            item(pair * 2 + 2, layer, 0)
                    else:
                        with eng.Fori(n0 + 1, n0 + B - 1) as n:
                            item(n, layer, 0)
                    item(n0 + B - 1, layer, 1)
            return run

        def q1_here(n, layer):
            return (layer == 0 and not (isinstance(n, int) and n == 0)) or (isinstance(n, int) and n == B)

        def added(g, i, which=ADDED):
            return len(which) * g + sum(a <= i for a in which)

        def exps(layer, g, i):
            return HALVES * g + sum((EXP_AT[layer][k], k) <= (EXP_AT[layer][i], i) for k in range(HALVES))

        def y_here(n):
            return not (isinstance(n, int) and n == 0)

        @block.sync
        def _(sp):
            for s in dma_signals:
                s.start(sp)

            def load_batch(b, slot):
                sp.dma_start(ctx_slot[slot][:, 0, :], ctxT[b, 0:P, :]).then_inc(ctx_in[slot].sem, 16)
                sp.dma_start(ctx_slot[slot][:, 1, :], ctxT[b, P:CD, :]).then_inc(ctx_in[slot].sem, 16)
                sp.dma_start(x_slot[slot][:, 0, :], xT[b, 0:P, :]).then_inc(x_in[slot].sem, 16)
                sp.dma_start(x_slot[slot][0:CT, 1, :], xT[b, P:C, :]).then_inc(x_in[slot].sem, 16)

            def const(dst, src, arrived=weights_in):
                sp.dma_start(dst, src).then_inc(arrived, 16)

            const(wkt, wk_text.rearrange("(a p) c -> p a c", p=P), keys_in)
            const(wki, wk_ip.rearrange("(a p) c -> p a c", p=P), keys_in)
            load_batch(0, 0)
            for layer in range(LAYERS):
                const(wq_sb[:, layer, 0, :], wq[layer, 0:P, :])
                const(wq_sb[0:CT, layer, 1, :], wq[layer, P:C, :])
            const(wvt, wv_text.rearrange("(a p) c -> p a c", p=P))
            const(wvi, wv_ip.rearrange("(a p) c -> p a c", p=P))
            const(id_f[:, :], ident)
            const(rows_sb[:, :], first_rows)
            for layer in range(LAYERS):
                const(wo_sb[:, layer, 0, :], wo[layer, 0:P, :])
                const(wo_sb[0:CT, layer, 1, :], wo[layer, P:C, :])
            const(bo_sb[:, :, :], bo)
            const(mask_sb[:, 0, :], mask)
            load_batch(1, 1)

            def store_batch(b, slot, load_next):
                for u, name in enumerate(UNITS):
                    if name == "s0":
                        if load_next:
                            sp.wait_ge(products.sem, products.at(b, pe_job["k1"]))
                            load_batch(b + 2, slot)
                        sp.wait_ge(dve_prep.sem, dve_prep.at(b, dve_job["semq1"]))
                        sp.dma_start(sem_q_dram[b], sem_q_out).then_inc(sem_q_stored.sem, 16)
                    sp.wait_ge(split_done.sem, split_done.at(b, u + 1))
                    done = unit_stored[u].sem
                    src = parts[u]
                    if name in ("s0", "s1"):
                        h = int(name[1])
                        sp.dma_start(sem_k_dram[b, :, :, h * L:(h + 1) * L], src).then_inc(done, 16)
                        if name == "s1":
                            sp.dma_start(sem_k32_dram[b], sem_k32_out).then_inc(sem_k32_stored.sem, 16)
                        continue
                    for r in range(PARTS):
                        if name in ("k0", "k1"):
                            dst = k_stack[int(name[1]), b, r, :, 0:P, :]
                            sp.dma_start(dst.rearrange("i c k -> c i k"), src).then_inc(done, 16)
                        elif name == "krem":
                            for layer in range(LAYERS):
                                dst = k_stack[layer, b, r, :, P:C, :]
                                sp.dma_start(dst.rearrange("i c k -> c i k"),
                                             src[layer * CT:(layer + 1) * CT]).then_inc(done, 16)
                        else:
                            dst = q_stack[0, b, :, r, 0:P, :]
                            sp.dma_start(dst.rearrange("j c k -> c j k"), src[:, :, 0:S]).then_inc(done, 16)
                            dst = q_stack[0, b, :, r, P:C, :]
                            sp.dma_start(dst.rearrange("j c k -> c j k"), src[0:CT, :, S:2 * S]).then_inc(done, 16)

            def load_kq(layer, b, g):
                sp.dma_start(ks[0:STACK, g, :, :], k_stack[layer, b].rearrange(
                    "j i (d h) k -> (j i d) h k", d=D)[:, HG * g:HG * g + HG, :]).then_inc(kq_in[g].sem, 16)
                sp.dma_start(qs[0:STACK, g, :, :], q_stack[layer, b].rearrange(
                    "j i (d h) k -> (j i d) h k", d=D)[:, HG * g:HG * g + HG, :]).then_inc(kq_in[g].sem, 16)

            def load_sem_q(b, slot):
                sp.dma_start(sem_q[slot], sem_q_dram[b]).then_inc(sem_q_in.sem, 16)

            def load_sem_k(b, slot):
                sp.dma_start(sem_k[slot], sem_k_dram[b]).then_inc(sem_k_in.sem, 16)
                sp.dma_start(sem_k32[slot], sem_k32_dram[b]).then_inc(sem_k_in.sem, 16)

            def m_rows(n, g):
                sp.wait_ge(m_row_out.sem, m_row_out.at(n, g + 1))
                sp.dma_start(qs[MROW:KROWS, g, :, :], mrow[:, :].rearrange("r (a k) -> r a k", a=1)
                             .broadcast_to((MR, HG, S))).then_inc(m_row_in.sem, 16)

            sp.wait_ge(zeroed, 2)
            sp.dma_start(ks[MROW:KROWS, :, :, :].rearrange("r g j k -> r (g j k)"), key_kind).then_inc(kinds_in, 16)
            for g in range(NG):
                sp.dma_start(vtile[:, g, :, :, :], value_ones).then_inc(kinds_in, 16)
            store_batch(0, 0, True)
            if B > 4:
                with sp.Fori(0, (B - 4) // 2) as pair:
                    store_batch(pair * 2 + 1, 1, True)
                    store_batch(pair * 2 + 2, 0, True)
            for s in (*unit_stored, sem_q_stored, sem_k32_stored):
                sp.wait_ge(s.sem, s.at(0, s.per))
            load_kq(0, 0, 0)
            load_kq(0, 0, 1)
            store_batch(B - 3, 1, True)
            load_kq(0, 0, 2)
            load_sem_q(0, 0)
            load_sem_k(0, 0)
            store_batch(B - 2, 0, False)
            load_kq(0, 0, 3)
            load_kq(0, 0, 4)
            store_batch(B - 1, 1, False)
            m_rows(0, 0)
            for s in (*unit_stored, sem_q_stored, sem_k32_stored):
                sp.wait_ge(s.sem, s.at(B - 1, s.per))

            def item(n, layer, slot):
                b = n - layer * B
                edge = isinstance(n, int)
                last_of_layer = edge and b == B - 1
                nxt = None if edge and n == ITEMS - 1 else ((1, 0) if last_of_layer else (layer, b + 1))
                for g in range(NG):
                    if g == 0 and layer == 0 and not last_of_layer:
                        sp.wait_ge(a_taken.sem, a_taken.at(n, 0))
                        if edge and n == 0:
                            sp.wait_ge(products.sem, products.at(B - 1, products.per))
                        load_sem_q(b + 1, 1 - slot)
                    if g >= 1 and nxt is not None:
                        sp.wait_ge(s_ready.sem, s_ready.at(n, HALVES * g))
                        if g == 1 and nxt[0] == 1:
                            sp.wait_ge(q1_stored.sem, q1_stored.at(nxt[1], 6))
                        load_kq(*nxt, g - 1)
                    elif g == 0 and not (edge and n == 0):
                        sp.wait_ge(s_ready.sem, s_ready.at(n, 0))
                        load_kq(layer, b, NG - 1)
                    if g < NG - 1:
                        m_rows(n, g + 1)
                    elif nxt is not None:
                        m_rows(n + 1, 0)
                    if g == 1 and layer == 0 and not last_of_layer:
                        load_sem_k(b + 1, 1 - slot)
                    if g == 3 and y_here(n):
                        store_y(n - 1, 0 if edge and n == B else layer)
                    if g == 3:
                        sp.wait_ge(y_ready.sem, y_ready.at(n, 0))
                        if layer == 1:
                            sp.wait_ge(y_stored.sem, y_stored.at(b, 1))
                        src = x if layer == 0 else x1_dram
                        sp.dma_start(res[:, :, :], src[b].rearrange("(t p) c -> p t c", p=P)).then_inc(res_in.sem, 16)
                    if g == 4 and q1_here(n, layer):
                        sp.wait_ge(q1_split.sem, q1_split.at(n - 1, 2))
                        for r in range(PARTS):
                            sp.dma_start(q_stack[1, n - 1, :, r, 0:P, :].rearrange("j c k -> c j k"),
                                         q_parts[:, :, 0:S]).then_inc(q1_stored.sem, 16)
                            sp.dma_start(q_stack[1, n - 1, :, r, P:C, :].rearrange("j c k -> c j k"),
                                         q_parts[0:CT, :, S:2 * S]).then_inc(q1_stored.sem, 16)

            def store_y(n, layer):
                sp.wait_ge(y_ready.sem, y_ready.at(n, 1))
                dst = (x1_dram if layer == 0 else out)[n - layer * B]
                sp.dma_start(dst.rearrange("(t p) c -> p t c", p=P), y_sb[:, :, :]).then_inc(y_stored.sem, 16)

            passes(item)(sp)
            store_y(ITEMS - 1, 1)
            sp.wait_ge(y_stored.sem, y_stored.at(ITEMS - 1, 1))

        @block.gpsimd
        def _(pool):
            for s in pool_signals:
                s.start(pool)
            pool.memset(mask_sb[:, 1, :], 1.0).then_inc(pool_init, 1)
            with pool.Fori(0, B) as b:
                for u, name in enumerate(UNITS):
                    pool.wait_ge(dve_prep.sem, dve_prep.at(b, dve_job[name + "_mid"]))
                    pool.tensor_tensor(parts[u][:, 2, :], rest[u], parts[u][:, 1, :],
                                       ALU.subtract).then_inc(split_done.sem, 1)

            def place_values(n, layer, b, g):
                cols = slice(HG * D * g, HG * D * (g + 1))

                def v(k0, k1):
                    return vals[:, layer, bass.ds(b, 1), k0:k1, cols].rearrange(
                        "p a k (h d) -> p (a k) h d", h=HG)
                pool.sem_inc(waited_pool, 1)
                pool.tensor_copy(vtile[:, g, 0:1, :, 0:D], v(0, 1))
                pool.tensor_copy(vtile[:, g, :, :, IPC:IPC + D], v(1, KC + 1)).then_inc(v_placed.sem, 1)

            def split_max(n, g):
                pool.wait_ge(a_taken.sem, a_taken.at(n, HG * (g + 1)))
                pool.wait_ge(m_turned.sem, m_turned.at(n, g))
                pool.sem_inc(waited_pool, 1)
                s = m_split.sem
                at = 4 * g

                def part(i):
                    return mpart[:, :, :, i, :]
                mxg = mx[:, g, :, :, :]
                r1 = mres[:, :, :, :]
                pool.tensor_copy(part(0), mxg).then_inc(s, 1)
                pool.wait_ge(m_split.sem, m_split.at(n, at + 1))
                pool.tensor_tensor(r1, mxg, part(0), ALU.subtract).then_inc(s, 1)
                pool.wait_ge(m_split.sem, m_split.at(n, at + 2))
                pool.sem_inc(waited_pool, 1)
                pool.tensor_copy(part(1), r1).then_inc(s, 1)
                pool.wait_ge(m_split.sem, m_split.at(n, at + 3))
                pool.tensor_tensor(part(2), r1, part(1), ALU.subtract).then_inc(s, 1)

            def join(n, layer, g):
                if isinstance(g, int) and g == 0:
                    pool.wait_ge(o_turned.sem, o_turned.at(n, 0))
                pool.wait_ge(weighed_ready.sem, weighed_ready.at(n, g + 1))
                image = weighed[:, :, 1, :].rearrange("p (t h) d -> p t h d", t=QT)
                pool.tensor_tensor(image, image, mask_sb[:, layer, :].rearrange("p (t a b) -> p t a b", a=1, b=1)
                                   .broadcast_to((P, QT, HG, D)), ALU.mult).then_inc(joined.sem, 1)
                pool.wait_ge(joined.sem, joined.at(n, 2 * g + 1))
                pool.tensor_tensor(o_sb[:, :, g, :, :], weighed[:, :, 0, :].rearrange("p (t h) d -> p t h d", t=QT),
                                   image, ALU.add).then_inc(joined.sem, 1)

            def add_semantic(n, g, i, slot):
                j, part = divmod(i, 2)
                if g == 0 and i == POOLED[0]:
                    pool.wait_ge(sem_k_in.sem, sem_k_in.at(n, 2))
                pool.wait_ge(s_copied.sem, s_copied.at(n, added(g, i, POOLED)))
                keys = slice(part * 512, (part + 1) * 512)
                pool.tensor_tensor(probs[:, (HG * g + j) % RING, keys], probs[:, (HG * g + j) % RING, keys],
                                   sem_k32[slot][:, keys], ALU.add).then_inc(s_pooled.sem, 1)

            pool.wait_ge(weights_in, N_WEIGHTS * 16)
            for s in (act_prep,):
                pool.wait_ge(s.sem, s.at(B - 1, act_job["s1_hi"]))
            pool.wait_ge(kinds_in, (1 + NG) * 16)
            for g in range(NG - 2):
                place_values(0, 0, 0, g)
            split_max(0, 0)

            def item(n, layer, slot):
                b = n - layer * B
                edge = isinstance(n, int)
                last_of_layer = edge and b == B - 1
                nxt = None if edge and n == ITEMS - 1 else ((1, 0) if last_of_layer else (layer, b + 1))
                for g in range(NG):
                    for at in range(STEPS):
                        if at == POOL_JOIN[layer] and g > 1:
                            join(n, layer, g - 2)
                        elif at == POOL_JOIN[layer] and not (edge and n == 0):
                            join(n - 1, 0 if edge and n == B else layer, g + NG - 2)
                        if at == POOL_SPLIT[layer] and g < NG - 1:
                            split_max(n, g + 1)
                        elif at == POOL_SPLIT[layer] and nxt is not None:
                            split_max(n + 1, 0)
                        if layer == 0 and at % 2 == 0 and at // 2 in POOLED:
                            add_semantic(n, g, at // 2, slot)
                        if at == POOL_PLACE[layer] and g < 2:
                            if not (edge and n == 0):
                                pool.wait_ge(pv_ready.sem, pv_ready.at(n - 1, g + NG - 1))
                            place_values(n, layer, b, g + NG - 2)
                        elif at == POOL_PLACE[layer] and nxt is not None:
                            pool.wait_ge(pv_ready.sem, pv_ready.at(n, g - 1))
                            place_values(n + 1, *nxt, g - 2)
                        if at == POOL_BIAS and g == 4:
                            pool.wait_ge(res_in.sem, res_in.at(n, 1))
                            pool.tensor_tensor(res[:, :, :], res[:, :, :], bo_sb[:, layer:layer + 1, :]
                                               .broadcast_to((P, QT, C)), ALU.add).then_inc(res_biased.sem, 1)
                        if at == POOL_Q1[0] and g == 3 and q1_here(n, layer):
                            pool.wait_ge(q1_rest.sem, q1_rest.at(n - 1, 1))
                            pool.wait_ge(q1_stored.sem, q1_stored.at(n - 1, 0))
                            pool.sem_inc(waited_pool, 1)
                            pool.tensor_copy(q_parts[:, 1, :], q_rest[:, :]).then_inc(q1_split.sem, 1)
                        if at == POOL_Q1[1] and g == 3 and q1_here(n, layer):
                            pool.wait_ge(q1_split.sem, q1_split.at(n - 1, 1))
                            pool.tensor_tensor(q_parts[:, 2, :], q_rest[:, :], q_parts[:, 1, :],
                                               ALU.subtract).then_inc(q1_split.sem, 1)

            passes(item)(pool)
            join(ITEMS - 1, 1, NG - 2)
            join(ITEMS - 1, 1, NG - 1)

        @block.tensor
        def _(pe):
            for s in pe_signals:
                s.start(pe)
            pe.wait_ge(keys_in, 2 * 16)

            def free_bank(b, name):
                names = list(pe_job)
                at = names.index(name)
                reader = last_reader[names[at - 8]]
                before = 0 if at >= 8 else 1
                if reader in act_job:
                    pe.wait_ge(act_prep.sem, act_prep.at(b, act_job[reader] - before * act_prep.per))
                else:
                    pe.wait_ge(dve_prep.sem, dve_prep.at(b, dve_job[reader] - before * dve_prep.per))

            def done(mm):
                mm.then_inc(products.sem, 1)

            pe.wait_ge(gram_zeroed, 1)
            def prepare(b, slot, turn):
                ctx_sb, x_sb = ctx_slot[slot], x_slot[slot]

                def keys(name, cols):
                    o = pbank[(pe_job[name] - 1) % 8]
                    free_bank(b, name)
                    for w, ks_ in ((wkt, slice(0, T)), (wki, slice(T, L))):
                        for a in range(2):
                            mm = pe.matmul(o[:, ks_], w[:, a, cols], ctx_sb[:, a, ks_],
                                           start=(a == 0), stop=(a == 1))
                    done(mm)

                def values(i):
                    name = f"v{i}"
                    o = pbank[(pe_job[name] - 1) % 8][:, 0:LAYERS * C]
                    free_bank(b, name)
                    w = wvt if i == 0 else wvi
                    c = max(i - 1, 0)
                    for a in range(2):
                        mm = pe.matmul(o, ctx_sb[:, a, c * P:(c + 1) * P], w[:, a, :],
                                       start=(a == 0), stop=(a == 1))
                    done(mm)

                pe.wait_ge(ctx_in[slot].sem, ctx_in[slot].at(turn, 2))
                keys("k0", slice(0, P))
                keys("krem", slice(2 * P, 3 * P))
                free_bank(b, "q")
                pe.wait_ge(weights_in, N_WEIGHTS * 16)
                pe.wait_ge(x_in[slot].sem, x_in[slot].at(turn, 2))
                o = pbank[pe_job["q"] - 1].rearrange("p (a s) -> p a s", a=2)
                for m in range(2):
                    pe.matmul(o[:, m, :], wq_sb[:, 0, 0, m * P:(m + 1) * P], x_sb[:, 0, :], start=True, stop=False)
                    mm = pe.matmul(o[:, m, :], wq_sb[0:CT, 0, 1, m * P:(m + 1) * P], x_sb[0:CT, 1, :],
                                   start=False, stop=True)
                done(mm)
                free_bank(b, "gram")
                for a in range(2):
                    mm = pe.matmul(pbank[pe_job["gram"] - 1][0:T, T:L], ctx_sb[:, a, 0:T], ctx_sb[:, a, T:L],
                                   start=(a == 0), stop=(a == 1))
                done(mm)
                free_bank(b, "txt")
                pe.wait_ge(act_prep.sem, act_prep.at(b, act_job["q_32"]))
                o = pbank[pe_job["txt"] - 1]
                for t in range(QT):
                    pe.matmul(o[:, t * T:(t + 1) * T], qt32[:, 0, t * P:(t + 1) * P], kt32[:, 0, :],
                              start=True, stop=False)
                    mm = pe.matmul(o[:, t * T:(t + 1) * T], qt32[0:CT, 1, t * P:(t + 1) * P],
                                   kt32[0:CT, 1, :], start=False, stop=True)
                done(mm)
                for i in range(KC + 1):
                    values(i)
                free_bank(b, "pT")
                pe.wait_ge(dve_prep.sem, dve_prep.at(b, dve_job["p1"]))
                for t in range(QT):
                    mm = pe.transpose(pbank[(pe_job["pT"] - 1) % 8][0:T, t * P:(t + 1) * P], p_txt[:, t, :], id_f[:, :])
                done(mm)
                keys("k1", slice(P, 2 * P))
                pe.wait_ge(act_prep.sem, act_prep.at(b, act_job["pT"]))
                for t in range(QT):
                    free_bank(b, f"semq{t}")
                    done(pe.matmul(pbank[4 + t][:, 0:L - T], pT_txt[:, t * P:(t + 1) * P], gram[:, T:L],
                                   start=True, stop=True))
                for h in range(2):
                    free_bank(b, f"s{h}")
                    for c in range(2):
                        k = 2 * h + c
                        mm = pe.matmul(pbank[6 + h][:, c * S:(c + 1) * S], gram[:, k * P:(k + 1) * P],
                                       pT_txt[:, :], start=True, stop=True)
                    done(mm)

            with pe.Fori(0, B // 2) as pair:
                prepare(pair * 2, 0, pair)
                prepare(pair * 2 + 1, 1, pair)

            pe.wait_ge(dve_prep.sem, dve_prep.at(B - 1, dve_job["k1_r"]))
            pe.wait_ge(id_b_ready, 1)
            pe.wait_ge(zeroed, 2)
            pe.wait_ge(kinds_in, (1 + NG) * 16)

            def by_query(n, g, i):
                if i == 0:
                    pe.wait_ge(kq_in[g].sem, kq_in[g].at(n, 2))
                j, t = divmod(i, QT)
                if t == 0:
                    pe.wait_ge(a_taken.sem, a_taken.at(n, HG * g + j - 1))
                mm = pe.matmul(by_query_bank[j % 2][:, t, :], qs[0:MROW, g, j, t * P:(t + 1) * P],
                               ks[0:MROW, g, j, :], start=True, stop=True)
                if t == QT - 1:
                    mm.then_inc(a_ready.sem, 1)

            def bank_read(n, layer, g, i):
                if layer == 0 and (i + 6) % 8 in POOLED:
                    pe.wait_ge(s_copied.sem, s_copied.at(n, added(g, i - 2, POOLED) if i >= 2
                                                         else added(g - 1, i + 6, POOLED)))
                elif layer == 0 and (i + 6) % 8 in ADDED:
                    pe.wait_ge(s_added.sem, s_added.at(n, added(g, i - 2) if i >= 2 else added(g - 1, i + 6)))
                else:
                    pe.wait_ge(probs_ready.sem, probs_ready.at(n, exps(layer, g, i - 2) if i >= 2
                                                               else exps(layer, g - 1, i + 6)))

            def by_key(n, layer, g, i, slot, turned=True):
                j, part = divmod(i, 2)
                o = by_key_bank[i % 2]
                here = layer == 0 and i not in ADDED + POOLED
                if i == 0:
                    pe.wait_ge(m_row_in.sem, m_row_in.at(n, g + 1))
                if g == 0 and here and i == min(k for k in range(HALVES) if k not in ADDED + POOLED):
                    pe.wait_ge(sem_k_in.sem, sem_k_in.at(n, 2))
                if i == TURN[layer] // 2 + 1 and turned:
                    pe.wait_ge(m_row_out.sem, m_row_out.at(n, g + 2))
                else:
                    bank_read(n, layer, g, i)
                for c in range(2):
                    k = 2 * part + c
                    mm = pe.matmul(o[:, c * S:(c + 1) * S], ks[0:KROWS, g, j, k * P:(k + 1) * P],
                                   qs[0:KROWS, g, j, :], start=(not here or c == 0), stop=not here,
                                   skip_group_check=here)
                if here:
                    for p in range(PARTS):
                        mm = pe.matmul(o[:, :], id_b[:, :], sem_k[slot][:, p, part * L:(part + 1) * L],
                                       start=False, stop=(p == PARTS - 1), skip_group_check=True)
                mm.then_inc(s_ready.sem, 1)

            def times_values(n, g, *chunks):
                if 0 in chunks:
                    pe.wait_ge(probs_ready.sem, probs_ready.at(n, HALVES * (g + 1)))
                    pe.wait_ge(weighed_ready.sem, weighed_ready.at(n, g))
                    pe.wait_ge(v_placed.sem, v_placed.at(n, g + 1))
                for c in chunks:
                    for j in range(HG):
                        mm = pe.matmul(pv_bank[VW * j:VW * (j + 1), 0:S], vtile[:, g, c, j, :],
                                       probs[:, (HG * g + j) % RING, c * S:(c + 1) * S],
                                       start=(c == 0), stop=(c == KC - 1))
                if KC - 1 in chunks:
                    mm.then_inc(pv_ready.sem, 1)

            def turn_values(n, g):
                pe.wait_ge(pv_copied.sem, pv_copied.at(n, g + 1))
                for t in range(QT):
                    mm = pe.transpose(pv_bank[:, S + t * P:S + (t + 1) * P], sums[:, g, t * P:(t + 1) * P], id_f[:, :])
                mm.then_inc(values_ready.sem, 1)

            def turn_max(n, g):
                pe.wait_ge(m_split.sem, m_split.at(n, 4 * (g + 1)))
                pe.wait_ge(m_row_out.sem, m_row_out.at(n, g))
                for t in range(QT):
                    mm = pe.transpose(turned_max[:, t * P:(t + 1) * P],
                                      mpart[:, t, :, :, :].rearrange("p a b c -> p (a b c)"), id_b[:, :])
                mm.then_inc(m_turned.sem, 1)

            def turn_o(n, layer):
                pe.wait_ge(joined.sem, joined.at(n, 2 * NG))
                pe.wait_ge(y_ready.sem, y_ready.at(n - 1, 1))
                if layer == 0:
                    pe.wait_ge(q1_rest.sem, q1_rest.at(n - 1, 1))
                for m, (c0, c1) in enumerate(((0, P), (P, C))):
                    for t in range(QT):
                        mm = pe.transpose(misc[0:c1 - c0, m * S + t * P:m * S + (t + 1) * P],
                                          o_sb[:, t, :, :, :].rearrange("p g h d -> p (g h d)")[:, c0:c1], id_f[:, :])
                mm.then_inc(o_turned.sem, 1)

            def project_out(n, layer):
                pe.wait_ge(oT_ready.sem, oT_ready.at(n, 2))
                for t in range(QT):
                    for m, rows in enumerate((P, CT)):
                        mm = pe.matmul(misc[:, t * C:(t + 1) * C], oT[0:rows, m, t * P:(t + 1) * P],
                                       wo_sb[0:rows, layer, m, :], start=(m == 0), stop=(m == 1))
                mm.then_inc(y_mm.sem, 1)

            def turn_y(n):
                pe.wait_ge(y_ready.sem, y_ready.at(n, 1))
                for m, (c0, c1) in enumerate(((0, P), (P, C))):
                    for t in range(QT):
                        mm = pe.transpose(misc[0:c1 - c0, m * S + t * P:m * S + (t + 1) * P], y_sb[:, t, c0:c1],
                                          id_f[:, :])
                mm.then_inc(y_turned.sem, 1)

            def project_q1(n):
                pe.wait_ge(yT_ready.sem, yT_ready.at(n, 2))
                for m in range(2):
                    o = misc[:, m * S:(m + 1) * S]
                    pe.matmul(o, wq_sb[:, 1, 0, m * P:(m + 1) * P], yT[:, 0, :], start=True, stop=False)
                    mm = pe.matmul(o, wq_sb[0:CT, 1, 1, m * P:(m + 1) * P], yT[0:CT, 1, :],
                                   start=False, stop=True)
                mm.then_inc(q1_mm.sem, 1)

            for i in range(QT * HG):
                by_query(0, 0, i)
            pe.wait_ge(dve_prep.sem, dve_prep.at(B - 1, dve_prep.per))
            for i in range(QT * HG):
                by_query(0, 1, i)
                if i == 3:
                    turn_max(0, 0)

            def item(n, layer, slot):
                edge = isinstance(n, int)
                final = edge and n == ITEMS - 1
                layer_before = 0 if edge and n == B else layer
                for g in range(NG):
                    ahead = (n, g + 2) if g + 2 < NG else (None if final else (n + 1, g + 2 - NG))
                    before = (n, g - 1) if g > 0 else (None if edge and n == 0 else (n - 1, NG - 1))
                    for at in range(STEPS):
                        if at % 2 == 0:
                            by_key(n, layer, g, at // 2, slot, turned=not (final and g == NG - 1))
                        if at == TURN[layer] and not (final and g == NG - 1):
                            bank_read(n, layer, g, at // 2 + 1)
                            if g < NG - 1:
                                turn_max(n, g + 1)
                            else:
                                turn_max(n + 1, 0)
                        if at == PE_TURN_VALUES[layer] and before:
                            turn_values(*before)
                        for a in range(HALVES):
                            if ahead and BESIDE[layer][a] == at:
                                by_query(*ahead, a)
                        if at == PE_TURN_O[layer] and g == 1 and y_here(n):
                            turn_o(n - 1, layer_before)
                        if before and at in PE_PV[layer]:
                            times_values(*before, *(c for c in range(KC) if PE_PV[layer][c] == at))
                        if at == PE_YT and g == 2 and q1_here(n, layer):
                            turn_y(n - 1)
                        if at == PE_Q1 and g == 2 and q1_here(n, layer):
                            project_q1(n - 1)
                        if at == PE_OUT[layer] and g == 1 and y_here(n):
                            project_out(n - 1, layer_before)

            passes(item)(pe)
            n = ITEMS - 1
            times_values(n, NG - 1, *range(KC))
            turn_values(n, NG - 1)
            turn_o(n, 1)
            project_out(n, 1)

        @block.scalar
        def _(act):
            for s in act_signals:
                s.start(act)
            act.wait_ge(weights_in, N_WEIGHTS * 16)
            act.activation(id_b[:, :], id_f[:, :], ACT.Copy).then_inc(id_b_ready, 1)

            with act.Fori(0, B) as b:
                def bank_of(name):
                    return pbank[(pe_job[name] - 1) % 8]

                def copy(name, dst, src, **kw):
                    return act.activation(dst, src, kw.pop("func", ACT.Copy), **kw).then_inc(act_prep.sem, 1)

                def high_part(u):
                    act.wait_ge(unit_stored[u].sem, unit_stored[u].at(b, 0))
                    copy("hi", parts[u][:, 0, :], bank_of(UNITS[u]))

                def values(i):
                    act.wait_ge(products.sem, products.at(b, pe_job[f"v{i}"]))
                    keep = {"scale": rows_sb[:, i:i + 1]} if i < 2 else {}
                    copy("v", vals[:, :, bass.ds(b, 1), i, :].rearrange("p l a c -> p (l a) c"),
                         bank_of(f"v{i}")[:, 0:LAYERS * C].rearrange("p (l c) -> p l c", l=LAYERS), **keep)

                act.wait_ge(products.sem, products.at(b, pe_job["k0"]))
                copy("k32", kt32[:, 0, :], bank_of("k0")[:, 0:T])
                high_part(0)
                act.wait_ge(products.sem, products.at(b, pe_job["krem"]))
                copy("k32", kt32[0:CT, 1, :], bank_of("krem")[0:CT, 0:T])
                high_part(1)
                act.wait_ge(products.sem, products.at(b, pe_job["q"]))
                copy("q32", qt32[:, :, :].rearrange("p a s -> p (a s)"), bank_of("q"))
                high_part(2)
                act.wait_ge(products.sem, products.at(b, pe_job["gram"]))
                copy("gram", gram[:, T:L], bank_of("gram")[0:T, T:L], scale=SEM_SCALE)
                values(0)
                act.wait_ge(dve_prep.sem, dve_prep.at(b, dve_job["nmax"]))
                for t in range(QT):
                    copy("e", e_txt[:, t, :], bank_of("txt")[:, t * T:(t + 1) * T], func=ACT.Exp,
                         bias=stat[:, 1, t:t + 1], scale=SCALE, accum_out=stat[:, 2, t:t + 1])
                for i in range(1, KC + 1):
                    values(i)
                act.wait_ge(products.sem, products.at(b, pe_job["pT"]))
                copy("pT", pT_txt[:, :], bank_of("pT")[0:T, 0:S])
                act.wait_ge(products.sem, products.at(b, pe_job["k1"]))
                high_part(3)
                for h in range(2):
                    act.wait_ge(products.sem, products.at(b, pe_job[f"s{h}"]))
                    act.wait_ge(sem_k32_stored.sem, sem_k32_stored.at(b, 0))
                    copy("s32", sem_k32_out[:, h * L:(h + 1) * L], bank_of(f"s{h}"))
                    high_part(4 + h)

            def exponentials(n, layer, g, i):
                j, part = divmod(i, 2)
                place = probs[:, (HG * g + j) % RING, part * 512:(part + 1) * 512]
                if layer == 0 and i in POOLED:
                    act.wait_ge(s_pooled.sem, s_pooled.at(n, added(g, i, POOLED)))
                    src = place
                elif layer == 0 and i in ADDED:
                    act.wait_ge(s_added.sem, s_added.at(n, added(g, i)))
                    src = place
                else:
                    act.wait_ge(s_ready.sem, s_ready.at(n, HALVES * g + i + 1))
                    act.wait_ge(pv_ready.sem, pv_ready.at(n, (HG * g + j - RING) // HG + 1))
                    src = by_key_bank[i % 2][:, :]
                act.activation(place, src, ACT.Exp, scale=SCALE).then_inc(probs_ready.sem, 1)

            def copy_scores(n, g, i):
                j, part = divmod(i, 2)
                act.wait_ge(s_ready.sem, s_ready.at(n, HALVES * g + i + 1))
                act.wait_ge(pv_ready.sem, pv_ready.at(n, (HG * g + j - RING) // HG + 1))
                act.activation(probs[:, (HG * g + j) % RING, part * 512:(part + 1) * 512], by_key_bank[i % 2][:, :],
                               ACT.Copy).then_inc(s_copied.sem, 1)

            def take_m_rows(n, g):
                act.wait_ge(m_turned.sem, m_turned.at(n, g + 1))
                act.wait_ge(m_row_in.sem, m_row_in.at(n, g))
                act.activation(mrow[:, :], turned_max, ACT.Copy).then_inc(m_row_out.sem, 1)

            def copy_pv(n, g):
                act.wait_ge(pv_ready.sem, pv_ready.at(n, g + 1))
                act.activation(sums[:, g, :], pv_bank[:, 0:S], ACT.Copy).then_inc(pv_copied.sem, 1)

            def take_oT(n):
                act.wait_ge(o_turned.sem, o_turned.at(n, 1))
                for m, rows in enumerate((P, CT)):
                    act.activation(oT[0:rows, m, :], misc[0:rows, m * S:(m + 1) * S], ACT.Copy)\
                        .then_inc(oT_ready.sem, 1)

            take_m_rows(0, 0)

            for s in (*unit_stored, sem_k32_stored):
                act.wait_ge(s.sem, s.at(B - 1, s.per))
            act.wait_ge(split_done.sem, split_done.at(B - 1, split_done.per))

            def item(n, layer, slot):
                edge = isinstance(n, int)
                for g in range(NG):
                    for at in range(STEPS):
                        if layer == 0 and at % 2 == 0 and at // 2 in POOLED:
                            copy_scores(n, g, at // 2)
                        for i in range(HALVES):
                            if EXP_AT[layer][i] == at:
                                exponentials(n, layer, g, i)
                        if at == ACT_TAKE[layer] and g < NG - 1:
                            take_m_rows(n, g + 1)
                        elif at == ACT_TAKE[layer] and not (edge and n == ITEMS - 1):
                            take_m_rows(n + 1, 0)
                        if at == ACT_COPY[layer] and g > 0:
                            copy_pv(n, g - 1)
                        elif at == ACT_COPY[layer] and not (edge and n == 0):
                            copy_pv(n - 1, NG - 1)
                        if at == ACT_OT and g == 1 and y_here(n):
                            take_oT(n - 1)
                        if at == ACT_YT and g == 2 and q1_here(n, layer):
                            act.wait_ge(y_turned.sem, y_turned.at(n - 1, 1))
                            for m, rows in enumerate((P, CT)):
                                act.activation(yT[0:rows, m, :], misc[0:rows, m * S:(m + 1) * S], ACT.Copy)\
                                    .then_inc(yT_ready.sem, 1)
                        if at == ACT_HI and g == 2 and q1_here(n, layer):
                            act.wait_ge(q1_mm.sem, q1_mm.at(n - 1, 1))
                            act.wait_ge(q1_stored.sem, q1_stored.at(n - 1, 0))
                            act.activation(q_parts[:, 0, :], misc[:, :], ACT.Copy).then_inc(q1_hi.sem, 1)

            passes(item)(act)
            copy_pv(ITEMS - 1, NG - 1)
            take_oT(ITEMS - 1)

        @block.vector
        def _(dve):
            for s in dve_signals:
                s.start(dve)
            dve.memset(gram[:, 0:T], 0.0).then_inc(gram_zeroed, 1)
            for t in (ks, qs):
                dve.memset(t[:, :, :, :].rearrange("p g j k -> p (g j k)").bitcast(F32), 0.0).then_inc(zeroed, 1)
            dve.wait_ge(weights_in, N_WEIGHTS * 16)
            with dve.Fori(0, B) as b:
                def bank_of(name):
                    return pbank[(pe_job[name] - 1) % 8]

                def take_rest(u):
                    name = UNITS[u]
                    dve.wait_ge(act_prep.sem, act_prep.at(b, act_job[name + "_hi"]))
                    dve.wait_ge(split_done.sem, split_done.at(b, u + 1 - split_done.per))
                    dve.tensor_tensor(rest[u], bank_of(name), parts[u][:, 0, :], ALU.subtract)\
                        .then_inc(dve_prep.sem, 1)
                    dve.wait_ge(dve_prep.sem, dve_prep.at(b, dve_job[name + "_r"]))
                    dve.tensor_copy(parts[u][:, 1, :], rest[u]).then_inc(dve_prep.sem, 1)

                for u in range(3):
                    take_rest(u)
                dve.wait_ge(products.sem, products.at(b, pe_job["txt"]))
                dve.tensor_reduce(stat[:, 0, :], bank_of("txt")[:, 0:QT * T].rearrange("p (t k) -> p t k", t=QT),
                                  AX, ALU.max).then_inc(dve_prep.sem, 1)
                dve.wait_ge(dve_prep.sem, dve_prep.at(b, dve_job["max"]))
                dve.tensor_scalar(stat[:, 1, :], stat[:, 0, :], -SCALE, None, ALU.mult).then_inc(dve_prep.sem, 1)
                dve.wait_ge(act_prep.sem, act_prep.at(b, act_job["e1"]))
                dve.reciprocal(stat[:, 3, :], stat[:, 2, :]).then_inc(dve_prep.sem, 1)
                dve.wait_ge(dve_prep.sem, dve_prep.at(b, dve_job["rsum"]))
                for t in range(QT):
                    dve.tensor_scalar(p_txt[:, t, :], e_txt[:, t, :], stat[:, 3, t:t + 1], None, ALU.mult)\
                        .then_inc(dve_prep.sem, 1)
                take_rest(3)
                dve.wait_ge(sem_q_stored.sem, sem_q_stored.at(b, 0))
                for t in range(QT):
                    dve.wait_ge(products.sem, products.at(b, pe_job[f"semq{t}"]))
                    dve.tensor_copy(sem_q_out[:, t, :], bank_of(f"semq{t}")[:, 0:L - T]).then_inc(dve_prep.sem, 1)
                for u in range(4, 6):
                    take_rest(u)

            def maxima(n, layer, g, j, slot, halves=(0, 1), discard=fused[:, :]):
                scores = by_query_bank[j % 2]
                if 0 in halves:
                    if layer == 0 and g == 0 and j == 0:
                        dve.wait_ge(sem_q_in.sem, sem_q_in.at(n, 1))
                    dve.wait_ge(a_ready.sem, a_ready.at(n, HG * g + j + 1))
                    dve.tensor_reduce(mx[:, g, :, 0, j], scores[:, :, 0:T], AX, ALU.max)
                    if layer == 0:
                        dve.wait_ge(a_taken.sem, a_taken.at(n, HG * g + j - 1))
                if layer == 0:
                    for t in halves:
                        f0 = (QT * j + t) % FUSED * (L - T)
                        dve.sem_inc(waited_dve, 1)
                        last = dve.tensor_tensor_reduce(discard[:, f0:f0 + L - T], scores[:, t, T:L], sem_q[slot][:, t, :],
                                                        1.0, -3.0e38, ALU.add, ALU.max, mx[:, g, t, 1, j:j + 1])
                else:
                    last = dve.tensor_reduce(mx[:, g, :, 1, j], scores[:, :, T:L], AX, ALU.max)
                if 1 in halves:
                    last.then_inc(a_taken.sem, 1)

            def weigh(n, g):
                dve.wait_ge(values_ready.sem, values_ready.at(n, g + 1))
                dve.reciprocal(inv[:, :, :, :], den_turned).then_inc(inv_ready.sem, 1)
                dve.wait_ge(joined.sem, joined.at(n, 2 * g))
                dve.wait_ge(inv_ready.sem, inv_ready.at(n, g + 1))
                dve.tensor_tensor(weighed[:, :, :, :], values_turned, inv[:, :, :, :].broadcast_to(
                    (P, QT * HG, 2, D)), ALU.mult).then_inc(weighed_ready.sem, 1)

            def add_semantic(n, g, i, slot):
                j, part = divmod(i, 2)
                if g == 0 and i == ADDED[0] and isinstance(n, int) and n == 0:
                    for s in (*unit_stored, sem_k32_stored):
                        dve.wait_ge(s.sem, s.at(B - 1, s.per))
                if g == 0 and i == ADDED[0]:
                    dve.wait_ge(sem_k_in.sem, sem_k_in.at(n, 2))
                dve.wait_ge(s_ready.sem, s_ready.at(n, HALVES * g + i + 1))
                dve.wait_ge(pv_ready.sem, pv_ready.at(n, (HG * g + j - RING) // HG + 1))
                keys = slice(part * 512, (part + 1) * 512)
                dve.tensor_tensor(probs[:, (HG * g + j) % RING, keys], by_key_bank[i % 2][:, :],
                                  sem_k32[slot][:, keys], ALU.add).then_inc(s_added.sem, 1)

            def finish(n, layer):
                dve.wait_ge(y_mm.sem, y_mm.at(n, 1))
                dve.wait_ge(res_biased.sem, res_biased.at(n, 1))
                dve.wait_ge(y_stored.sem, y_stored.at(n, 0))
                dve.tensor_tensor(y_sb[:, :, :].rearrange("p t c -> p (t c)"), misc[:, 0:QT * C],
                                  res[:, :, :].rearrange("p t c -> p (t c)"), ALU.add).then_inc(y_ready.sem, 1)

            def take_q1_rest(n):
                dve.wait_ge(q1_hi.sem, q1_hi.at(n, 1))
                dve.wait_ge(q1_split.sem, q1_split.at(n, 0))
                dve.tensor_tensor(q_rest[:, :], misc[:, :], q_parts[:, 0, :], ALU.subtract)\
                    .then_inc(q1_rest.sem, 1)

            for g in range(2):
                for j in range(HG):
                    maxima(0, 0, g, j, 0, discard=sums[:, 0:4, :].rearrange("p a b -> p (a b)").bitcast(BF16))
            dve.wait_ge(sem_q_stored.sem, sem_q_stored.at(B - 1, 1))

            def item(n, layer, slot):
                edge = isinstance(n, int)
                final = edge and n == ITEMS - 1
                next_layer = 1 if edge and n == B - 1 else layer
                for g in range(NG):
                    ahead = (n, layer, g + 2) if g + 2 < NG else (None if final else (n + 1, next_layer, g + 2 - NG))
                    before = (n, g - 1) if g > 0 else (None if edge and n == 0 else (n - 1, NG - 1))
                    for at in range(STEPS):
                        if layer == 0 and at % 2 == 0 and at // 2 in ADDED:
                            add_semantic(n, g, at // 2, slot)
                        for half in range(QT * HG):
                            if ahead and ahead[1] == 0 and DVE_MAX[0][half] == at:
                                maxima(*ahead, half // 2, slot if g + 2 < NG else 1 - slot, (half % 2,))
                            elif ahead and ahead[1] == 1 and half < HG and DVE_MAX[1][half] == at:
                                maxima(*ahead, half, 0)
                        if at == DVE_FINISH and g == 2 and y_here(n):
                            finish(n - 1, 0 if edge and n == B else layer)
                        if at == DVE_WEIGH[layer] and before:
                            weigh(*before)
                        if at == DVE_REST and g == 2 and q1_here(n, layer):
                            take_q1_rest(n - 1)

            passes(item)(dve)
            weigh(ITEMS - 1, NG - 1)
            finish(ITEMS - 1, 1)


def kernel(x, ctx_2048, fside_S_0, L0_xattn_Wq, L0_xattn_Wk, L0_xattn_Wv, L0_xattn_Wk_ip, L0_xattn_Wv_ip,
           L0_xattn_Wout, L0_xattn_bout, L1_xattn_Wq, L1_xattn_Wk, L1_xattn_Wv, L1_xattn_Wk_ip,
           L1_xattn_Wv_ip, L1_xattn_Wo, L1_xattn_bo):
    import numpy as np
    import concourse.bacc as bacc
    from concourse.bass_utils import run_bass_kernel_spmd

    f = np.float32

    def dims_first(w):
        return np.asarray(w).reshape(w.shape[0], H, D).transpose(0, 2, 1).reshape(w.shape[0], C)

    def side_by_side(w0, w1):
        w0, w1 = dims_first(w0), dims_first(w1)
        pad = np.zeros((CD, 3 * P - 2 * C), f)
        return np.concatenate([w0[:, :P], w1[:, :P], w0[:, P:], w1[:, P:], pad], axis=1)

    wq = np.zeros((LAYERS, C, 2 * P), f)
    wq[0, :, :C] = dims_first(L0_xattn_Wq)
    wq[1, :, :C] = dims_first(np.asarray(L1_xattn_Wq).T)
    kind = np.zeros((2, PARTS, HG, NG, HG, L), f)
    for h in range(HG):
        kind[0, :, h, :, h, :T] = -1
        kind[1, :, h, :, h, T:] = -1
    ones = np.zeros((P, KC, VW), f)
    ones[:T, 0, D] = 1
    ones[T:, 0, IPC + D] = 1
    ones[:, 1:, IPC + D] = 1
    first_rows = np.zeros((P, 2), f)
    first_rows[:T, 0] = 1
    first_rows[T:, 1] = 1
    arrays = {
        "x": np.asarray(x),
        "xT": np.asarray(x).transpose(0, 2, 1),
        "ctxT": np.asarray(ctx_2048).transpose(0, 2, 1),
        "mask": np.asarray(fside_S_0).reshape(QT, P).T,
        "wk_text": side_by_side(L0_xattn_Wk, np.asarray(L1_xattn_Wk).T),
        "wk_ip": side_by_side(L0_xattn_Wk_ip, np.asarray(L1_xattn_Wk_ip).T),
        "wv_text": np.concatenate([np.asarray(L0_xattn_Wv), np.asarray(L1_xattn_Wv).T], axis=1),
        "wv_ip": np.concatenate([np.asarray(L0_xattn_Wv_ip), np.asarray(L1_xattn_Wv_ip).T], axis=1),
        "wq": wq,
        "wo": np.stack([np.asarray(L0_xattn_Wout), np.asarray(L1_xattn_Wo).T]),
        "bo": np.tile(np.stack([np.asarray(L0_xattn_bout), np.asarray(L1_xattn_bo)]), (P, 1, 1)),
        "ident": np.eye(P, dtype=f),
        "key_kind": kind.reshape(MR, H * L).astype(mybir.dt.np(BF16)),
        "value_ones": np.repeat(ones[:, :, None], HG, axis=2),
        "first_rows": first_rows,
    }
    arrays = {k: np.ascontiguousarray(v) for k, v in arrays.items()}
    nc = bacc.Bacc("TRN2", target_bir_lowering=False, num_devices=1)
    args = [nc.dram_tensor(k, v.shape, mybir.dt.from_np(v.dtype), kind="ExternalInput").ap()
            for k, v in arrays.items()]
    out = nc.dram_tensor("out", (B, S, C), F32, kind="ExternalOutput").ap()
    build(nc, *args, out)
    r = run_bass_kernel_spmd(nc, [arrays], core_ids=[0])
    return r.results[0]["out"]
```
